# Optimizing a Trainium2 kernel written in Bass

```python
import numpy as np
import jax
import jax.numpy as jnp

def _softmax(x, axis=-1):
    return jax.nn.softmax(x, axis=axis)

def _gelu(x):
    return jax.nn.gelu(x, approximate=True)

def _silu(x):
    return jax.nn.silu(x)

def _sigmoid(x):
    return jax.nn.sigmoid(x)

def _layernorm(x, axis=-1, eps=1e-05):
    m = jnp.mean(x, axis=axis, keepdims=True)
    v = jnp.var(x, axis=axis, keepdims=True)
    return (x - m) / jnp.sqrt(v + eps)

def _scatter_add(tgt, idx, src, axis=0):
    return tgt.at[idx].add(src)

def _segment_sum(src, seg, n):
    return jax.ops.segment_sum(src, seg, n)
kernel_name = 'mk_prb_d1_jaxref_r4_a14903'

def setup_inputs(seed: int=0):
    np.random.seed(seed)
    _w = jnp.asarray

    def _L0_attn_setup():
        import jax, jax.numpy as jnp
        import numpy as np
        B_SZ, SEQ = (2, 512)
        D_MODEL, D_STATE, D_CONV = (256, 16, 4)
        D_INPUT, D_OUTPUT = (256, 256)
        D_INNER = 2 * D_MODEL
        DT_RANK = D_MODEL // 16
        key = jax.random.key(seed)
        ks = jax.random.split(key, 8)

        def rn(k, shape, scale):
            return (jax.random.normal(k, shape) * scale).astype(jnp.float32)
        return {'x': rn(ks[0], (B_SZ, SEQ, D_INPUT), 1.0), 'fc1_w': rn(ks[1], (D_MODEL, D_INPUT), D_INPUT ** (-0.5)), 'fc1_b': jnp.zeros((D_MODEL,), jnp.float32), 'in_proj_w': rn(ks[2], (2 * D_INNER, D_MODEL), D_MODEL ** (-0.5)), 'conv_w': rn(ks[3], (D_INNER, D_CONV), D_CONV ** (-0.5)), 'conv_b': jnp.zeros((D_INNER,), jnp.float32), 'x_proj_w': rn(ks[4], (DT_RANK + 2 * D_STATE, D_INNER), D_INNER ** (-0.5)), 'dt_proj_w': rn(ks[5], (D_INNER, DT_RANK), DT_RANK ** (-0.5)), 'dt_proj_b': jnp.full((D_INNER,), -4.6, jnp.float32), 'A_log': jnp.log(jnp.broadcast_to(jnp.arange(1, D_STATE + 1, dtype=jnp.float32), (D_INNER, D_STATE))), 'D': jnp.ones((D_INNER,), jnp.float32), 'out_proj_w': rn(ks[6], (D_MODEL, D_INNER), D_INNER ** (-0.5)), 'fc2_w': rn(ks[7], (D_OUTPUT, D_MODEL), D_MODEL ** (-0.5)), 'fc2_b': jnp.zeros((D_OUTPUT,), jnp.float32)}
    _L0_attn_in = _L0_attn_setup()

    def _L0_ffn_setup():
        import jax, jax.numpy as jnp
        import numpy as np
        B, S, D = (4, 512, 256)
        O = 256
        E = 8
        K = 2
        key = jax.random.key(seed)
        k1, k2, k3, k4, k5 = jax.random.split(key, 5)
        scale = 1.0 / np.sqrt(D)
        x = jax.random.normal(k1, (B, S, D), dtype=jnp.float32)
        We = jax.random.uniform(k2, (E, D, O), dtype=jnp.float32, minval=-scale, maxval=scale)
        be = jax.random.uniform(k3, (E, O), dtype=jnp.float32, minval=-scale, maxval=scale)
        Wg = jax.random.uniform(k4, (D, E), dtype=jnp.float32, minval=-scale, maxval=scale)
        bg = jax.random.uniform(k5, (E,), dtype=jnp.float32, minval=-scale, maxval=scale)
        return {'x': x, 'We': We, 'be': be, 'Wg': Wg, 'bg': bg}
    _L0_ffn_in = _L0_ffn_setup()
    _d = {'L0_attn_x': _L0_attn_in['x'], 'L0_attn_fc1_w': _L0_attn_in['fc1_w'], 'L0_attn_fc1_b': _L0_attn_in['fc1_b'], 'L0_attn_in_proj_w': _L0_attn_in['in_proj_w'], 'L0_attn_conv_w': _L0_attn_in['conv_w'], 'L0_attn_conv_b': _L0_attn_in['conv_b'], 'L0_attn_x_proj_w': _L0_attn_in['x_proj_w'], 'L0_attn_dt_proj_w': _L0_attn_in['dt_proj_w'], 'L0_attn_dt_proj_b': _L0_attn_in['dt_proj_b'], 'L0_attn_A_log': _L0_attn_in['A_log'], 'L0_attn_D': _L0_attn_in['D'], 'L0_attn_out_proj_w': _L0_attn_in['out_proj_w'], 'L0_attn_fc2_w': _L0_attn_in['fc2_w'], 'L0_attn_fc2_b': _L0_attn_in['fc2_b'], 'L0_ffn_We': _L0_ffn_in['We'], 'L0_ffn_be': _L0_ffn_in['be'], 'L0_ffn_Wg': _L0_ffn_in['Wg'], 'L0_ffn_bg': _L0_ffn_in['bg']}
    _x0 = _d['L0_attn_x']
    _d['L0_attn_x'] = jax.random.normal(jax.random.fold_in(jax.random.key(seed), 1), (8, 2048, 256), dtype=_x0.dtype)
    del _x0
    return _d

def reference(L0_attn_x, L0_attn_fc1_w, L0_attn_fc1_b, L0_attn_in_proj_w, L0_attn_conv_w, L0_attn_conv_b, L0_attn_x_proj_w, L0_attn_dt_proj_w, L0_attn_dt_proj_b, L0_attn_A_log, L0_attn_D, L0_attn_out_proj_w, L0_attn_fc2_w, L0_attn_fc2_b, L0_ffn_We, L0_ffn_be, L0_ffn_Wg, L0_ffn_bg):

    def _L0_attn_ref(x, fc1_w, fc1_b, in_proj_w, conv_w, conv_b, x_proj_w, dt_proj_w, dt_proj_b, A_log, D, out_proj_w, fc2_w, fc2_b):
        import jax, jax.numpy as jnp
        import numpy as np
        B_SZ, SEQ = (2, 512)
        D_MODEL, D_STATE, D_CONV = (256, 16, 4)
        D_INPUT, D_OUTPUT = (256, 256)
        D_INNER = 2 * D_MODEL
        DT_RANK = D_MODEL // 16
        B, L, _ = x.shape
        d_inner, d_conv = conv_w.shape
        d_state = A_log.shape[1]
        dt_rank = dt_proj_w.shape[1]
        h = x @ fc1_w.T + fc1_b
        xz = h @ in_proj_w.T
        xc, z = jnp.split(xz, 2, axis=-1)
        xp = jnp.pad(xc, ((0, 0), (d_conv - 1, 0), (0, 0)))
        u = sum((xp[:, w:w + L, :] * conv_w[:, w] for w in range(d_conv))) + conv_b
        u = jax.nn.silu(u)
        x_dbl = u @ x_proj_w.T
        dt_low, Bm, Cm = jnp.split(x_dbl, [dt_rank, dt_rank + d_state], axis=-1)
        dt = jax.nn.softplus(dt_low @ dt_proj_w.T + dt_proj_b)
        A = -jnp.exp(A_log)

        def step(hstate, t):
            dt_t, B_t, C_t, u_t = t
            dA = jnp.exp(dt_t[..., None] * A)
            hstate = dA * hstate + (dt_t * u_t)[..., None] * B_t[:, None, :]
            y_t = jnp.einsum('bdn,bn->bd', hstate, C_t)
            return (hstate, y_t)
        h0 = jnp.zeros((B, d_inner, d_state), x.dtype)
        xs = (jnp.swapaxes(dt, 0, 1), jnp.swapaxes(Bm, 0, 1), jnp.swapaxes(Cm, 0, 1), jnp.swapaxes(u, 0, 1))
        _, ys = jax.lax.scan(step, h0, xs)
        y = jnp.swapaxes(ys, 0, 1) + u * D
        y = y * jax.nn.silu(z)
        out = y @ out_proj_w.T
        return out @ fc2_w.T + fc2_b

    def _L0_ffn_ref(x, We, be, Wg, bg):
        import jax, jax.numpy as jnp
        import numpy as np
        B, S, D = (4, 512, 256)
        O = 256
        E = 8
        K = 2
        b, s, d = x.shape
        x_flat = x.reshape(-1, d)
        gates = jax.nn.softmax(x_flat @ Wg + bg, axis=-1)
        topk_gates, topk_idx = jax.lax.top_k(gates, K)
        topk_gates = topk_gates / jnp.sum(topk_gates, axis=1, keepdims=True)
        expert_out = jnp.einsum('nd,edo->neo', x_flat, We) + be
        selected = jnp.take_along_axis(expert_out, topk_idx[:, :, None], axis=1)
        out = jnp.sum(selected * topk_gates[:, :, None], axis=1)
        return out.reshape(b, s, -1)
    x = L0_attn_x
    xn = _layernorm(x, axis=-1)
    x = x + _L0_attn_ref(xn, L0_attn_fc1_w, L0_attn_fc1_b, L0_attn_in_proj_w, L0_attn_conv_w, L0_attn_conv_b, L0_attn_x_proj_w, L0_attn_dt_proj_w, L0_attn_dt_proj_b, L0_attn_A_log, L0_attn_D, L0_attn_out_proj_w, L0_attn_fc2_w, L0_attn_fc2_b) + _L0_ffn_ref(xn, L0_ffn_We, L0_ffn_be, L0_ffn_Wg, L0_ffn_bg)
    return x

_drawn_inputs = setup_inputs


def setup_inputs(seed=0):
    import zlib

    import numpy as np

    out = dict(_drawn_inputs(seed))
    spreads = {'L0_attn_fc1_b': (0.0, 0.1),
     'L0_attn_conv_b': (0.0, 0.1),
     'L0_attn_dt_proj_b': (-4.599999904632568, 0.6),
     'L0_attn_D': (1.0, 0.2),
     'L0_attn_fc2_b': (0.0, 0.1)}
    factors = {}
    for name, (base, spread) in spreads.items():
        noise = np.random.default_rng([zlib.crc32(name.encode()), seed]).standard_normal(out[name].shape)
        drawn = base * np.exp(spread * noise) if base else spread * noise
        out[name] = jnp.asarray(drawn.astype(out[name].dtype))
    for name, factor in factors.items():
        out[name] = (out[name] * factor).astype(out[name].dtype)
    return out
```

```python
import concourse.bass as bass
from concourse import mybir
from contextlib import ExitStack

P = 128
F32 = mybir.dt.float32
ALU = mybir.AluOpType
ACT = mybir.ActivationFunctionType
AX_X = mybir.AxisListType.X

EPS = 1e-5
BIG = 3.0e38
EXP_CAP = 40.0
RATIO = 2

Q_STATS = 2
Q_NORM = 4
Q_XNT = (6, 7)
Q_GT = 8
Q_YG = (9, 10, 11, 12)
Q_LOGIT = 13
Q_XC = (14, 15, 16, 17)
Q_OUT = (18, 20, 22, 24)
Q_Z = (19, 21, 23, 25)
Q_CONV = (26, 29, 32, 35)
Q_SILU = 38
Q_XD = 41
Q_BC = 43
Q_DT = (44, 45, 46, 47)
Q_MIN = 48
Q_SP = 49
Q_MAX = 51
Q_DTU = 52
Q_DUT = (57, 58, 59, 60)
Q_MOE = (27, 28, 30, 31, 33, 34, 37, 38, 39, 40, 42, 48, 50, 52, 54, 56)

FRONT = ([("xnT", k) for k in range(2)] + [("logit", 0)] + [("xc", k) for k in range(4)]
         + [("z", k) for k in range(4)] + [("conv", k) for k in range(4)] + [("xd", 0), ("bc", 0)]
         + [("dt", k) for k in range(4)] + [("duT", k) for k in range(4)])
BACK = [("gT", 0)] + [("yg", k) for k in range(4)] + [("out", k) for k in range(4)]
SIDE = BACK + [("moe", k) for k in range(16)]
NF, NB, NS = len(FRONT), len(BACK), len(SIDE)
FRONT_AT = {job: i for i, job in enumerate(FRONT)}
SIDE_AT = {job: i for i, job in enumerate(SIDE)}


class Chunk:

    def __init__(self, turn, part):
        self.turn, self.part = turn, part
        self.index = turn * RATIO + part

    def count(self, per, more=0):
        return self.turn * (RATIO * per) + (self.part * per + more)

    def step(self, by):
        part = self.part + by
        return Chunk(self.turn + part // RATIO, part % RATIO)

    def half(self, per, more):
        return self.turn * per + (self.part * per + more) // 2

    def is_int(self):
        return isinstance(self.turn, int)


def wait(eng, sem, value):
    if isinstance(value, int) and value <= 0:
        return
    eng.wait_ge(sem, value)


def apart(eng, passed):
    eng.nop().then_inc(passed, 1)


def mamba_moe_kernel(nc, x, fc1_w, fc1_b, in_proj_w, conv_w, conv_b, x_proj_w, dt_proj_w, dt_proj_b,
                     A_log, D, out_proj_w, fc2_w, fc2_b, We, be, Wg, bg, out):
    B, L, DM = x.shape
    DI, NSTATE = A_log.shape
    TAPS = conv_w.shape[1]
    R = dt_proj_w.shape[1]
    XD = R + 2 * NSTATE
    NE = Wg.shape[1]
    KT, DT, ET = DM // P, DI // P, 2 * DI // P
    CT = 512
    TB = CT // P
    CHUNKS = B * L // CT
    PER_BATCH = L // CT
    STEPS = NSTATE * DT
    HIST = TAPS - 1
    assert DM == 256 and DI == 512 and TB == DT == 4 and PER_BATCH == 2 * RATIO and CHUNKS % RATIO == 0
    TURNS = CHUNKS // RATIO

    x_v = x.rearrange("b (c t p) d -> (b c) p t d", t=TB, p=P)
    out_v = out.rearrange("b (c t p) d -> (b c) p t d", t=TB, p=P)

    with ExitStack() as ctx:
        def sb(name, shape):
            return ctx.enter_context(nc.sbuf_tensor(name, shape, F32))

        def sem(name):
            return ctx.enter_context(nc.semaphore(name))

        ident = sb("ident", [P, P])
        w_xz = sb("w_xz", [P, KT, 2 * DI])
        b_xz = sb("b_xz", [P, ET])
        w_conv = sb("w_conv", [P, DT, TAPS, P])
        w_xd = sb("w_xd", [P, DT, XD])
        w_dt = sb("w_dt", [R, DI])
        w_out = sb("w_out", [P, DT, DM])
        w_exp = sb("w_exp", [P, KT, NE * DM])
        b_out = sb("b_out", [NE + 1, DM])
        w_gate = sb("w_gate", [P, KT, NE])
        b_gate = sb("b_gate", [P, TB, NE])
        prio = sb("prio", [P, TB, NE])
        cw = sb("cw", [P, DT, TAPS])
        cb = sb("cb", [P, DT])
        b_dt = sb("b_dt", [P, DT])
        d_col = sb("d_col", [P, DT])
        f1b = sb("f1b", [P, KT])
        A = sb("A", [P, DT, NSTATE])
        half_neg = sb("half_neg", [P, TB])

        xin = sb("xin", [P, 2, TB, DM])
        xc = sb("xc", [P, DT, HIST + CT])
        xn = xc[:, :, 0:DM]
        xnT = sb("xnT", [P, 2, KT, CT])
        u = sb("u", [P, 2, DT, CT])
        sz = sb("sz", [P, 2, DT, CT])
        dt = sb("dt", [P, 2, DT, CT])
        wide = sb("wide", [P, DT, CT])
        duT = sb("duT", [P, 2, TB, DI])
        bc = sb("bc", [P, 2, TB, XD])
        xdT = sb("xdT", [XD, CT])
        gates = sb("gates", [P, 2, TB, NE + 1])
        gT = sb("gT", [NE + 1, CT])
        acc = sb("acc", [P, TB, DM])
        stat = sb("stat", [P, TB, 6])
        mv = sb("mv", [P, TB, 2])
        rstd = sb("rstd", [P, 3, TB])
        gw = sb("gw", [P, 8, TB, NE])
        gs = sb("gs", [P, 8, TB])
        hist = sb("hist", [P, 3, DT, HIST])
        state = sb("state", [P, 3, NSTATE, DT])
        xb = sb("xb", [P, 2, TB, DI])
        dA = sb("dA", [P, DT, CT])
        h = sb("h", [P, 2, DT, CT])
        yT = sb("yT", [P, 2, TB, DI])

        s_inp = xb[:, 0, :, :].rearrange("p a b -> p (a b)")[:, 0:ET * DM].rearrange("p (e m) -> p e m", m=DM)
        s_fc1 = xb[:, 1, 0, :].rearrange("p (m i) -> p m i", m=KT)
        s_fc2 = xb[:, 1, 1, :].rearrange("p (o m) -> p o m", o=KT)
        s_outp = xb[:, 1, 2:4, :]
        s_xp = dA[0:XD, 0, :]
        s_dt = dA[:, 1, 0:DT * R].rearrange("p (a r) -> p a r", a=DT)
        s_inT = h[:, 0, :, :].rearrange("p a b -> p (a b)").rearrange("p (m e) -> p m e", m=KT)
        s_fc2T = h[:, 1, 0, :].rearrange("p (m o) -> p m o", m=KT)

        def psum(name):
            return ctx.enter_context(nc.psum_tensor(name, [P, 512], F32))

        ps_x = [psum(f"ps_x{i}") for i in range(2)]
        ps_h = [psum(f"ps_h{i}") for i in range(2)]
        ps_f = [psum(f"ps_f{i}") for i in range(2)]
        ps_s = [psum(f"ps_s{i}") for i in range(2)]

        passed = sem("passed")
        w_loaded = sem("w_loaded")
        consts_set = sem("consts_set")
        A_exp = sem("A_exp")
        prep_filled = sem("prep_filled")
        prep_copied = sem("prep_copied")
        x_loaded = [sem(f"x_loaded{i}") for i in range(RATIO)]
        out_stored = sem("out_stored")
        ln_chain = sem("ln_chain")
        norm_chain = sem("norm_chain")
        gate_chain = sem("gate_chain")
        top_ready = sem("top_ready")
        e2_ready = sem("e2_ready")
        front_filled = sem("front_filled")
        front_freed = [sem(f"front_freed{i}") for i in range(2)]
        side_filled = sem("side_filled")
        side_freed = [sem(f"side_freed{i}") for i in range(2)]
        xnT_ready = sem("xnT_ready")
        hist_set = sem("hist_set")
        hist_saved = sem("hist_saved")
        xc_ready = sem("xc_ready")
        pre_ready = sem("pre_ready")
        silu_ready = sem("silu_ready")
        xd_ready = sem("xd_ready")
        bc_ready = sem("bc_ready")
        v_ready = sem("v_ready")
        vmin_ready = sem("vmin_ready")
        sp_chain = sem("sp_chain")
        dt_ready = sem("dt_ready")
        du_ready = sem("du_ready")
        duT_ready = sem("duT_ready")
        xb_ready = sem("xb_ready")
        x_filled = sem("x_filled")
        dA_ready = sem("dA_ready")
        scan_done = sem("scan_done")
        state_saved = sem("state_saved")
        h_filled = sem("h_filled")
        y_added = sem("y_added")
        gT_ready = sem("gT_ready")
        yd_ready = sem("yd_ready")
        yg_ready = sem("yg_ready")
        moe_added = sem("moe_added")
        out_ready = sem("out_ready")

        N_LOADS = 15 + KT + TB
        N_CONSTS = 5 + NE + 1 + DT * TAPS + 1
        gates_ready = sem("gates_ready")

        def turn_in(m, half):
            def fill(pe, bank):
                for i in range(4):
                    last = pe.transpose(bank[:, i * P:(i + 1) * P], s_inp[:, 4 * half + i, m * P:(m + 1) * P], ident[:])
                return last
            return fill, s_inT[:, m, half * 512:(half + 1) * 512], lambda bank: bank[:]

        def turn_fc2(m):
            def fill(pe, bank):
                for o in range(KT):
                    last = pe.transpose(bank[:, o * P:(o + 1) * P], s_fc2[:, o, m * P:(m + 1) * P], ident[:])
                return last
            return fill, s_fc2T[:, m, :], lambda bank: bank[:, 0:DM]

        def turn_xd(pe, bank):
            for i in range(DT):
                last = pe.transpose(bank[:, i * XD:(i + 1) * XD], s_xp[:, i * P:(i + 1) * P], ident[0:XD, 0:XD])
            return last

        def turn_dt(pe, bank):
            for i in range(DT):
                last = pe.transpose(bank[0:R, i * P:(i + 1) * P], s_dt[:, i, :], ident[:])
            return last

        def join_in(i, half):
            def fill(pe, bank):
                pe.wait_ge(prep_copied, 4)
                for m in range(KT):
                    last = pe.matmul(bank[:], s_fc1[:, m, i * P:(i + 1) * P], s_inT[:, m, half * 512:(half + 1) * 512],
                                     start=m == 0, stop=m == KT - 1)
                return last
            return fill, w_xz[:, i, half * 512:(half + 1) * 512], lambda bank: bank[:]

        def join_bias(pe, bank):
            for e in range(ET):
                for m in range(KT):
                    last = pe.matmul(bank[:, e:e + 1], s_inT[:, m, e * P:(e + 1) * P], f1b[:, m:m + 1],
                                     start=m == 0, stop=m == KT - 1)
            return last

        def join_out(a):
            def fill(pe, bank):
                pe.wait_ge(prep_copied, 6)
                for m in range(KT):
                    last = pe.matmul(bank[:, 0:DM], s_outp[:, m, a * P:(a + 1) * P], s_fc2T[:, m, :],
                                     start=m == 0, stop=m == KT - 1)
                return last
            return fill, w_out[:, a, :], lambda bank: bank[:, 0:DM]

        prep_jobs = ([turn_in(m, half) for m in range(KT) for half in range(2)] + [turn_fc2(m) for m in range(KT)]
                     + [(turn_xd, w_xd[:], lambda bank: bank[:, 0:DT * XD].rearrange("p (a x) -> p a x", a=DT)),
                        (turn_dt, w_dt[:], lambda bank: bank[0:R, :])]
                     + [join_in(i, half) for i in range(KT) for half in range(2)]
                     + [(join_bias, b_xz[:], lambda bank: bank[:, 0:ET])] + [join_out(a) for a in range(DT)])

        block = ctx.enter_context(nc.Block())

        N_LN = 2 * TB
        N_NORM = 4 + TB
        N_GATE = 17

        def side_count(ck, job, more=0):
            return ck.count(NS, SIDE_AT[job] - NB + more)

        def side_bank(ck, job):
            return (ck.part * NS + SIDE_AT[job] - NB) % 2

        def side_turn(ck, job):
            return ck.half(NS, SIDE_AT[job] - NB)

        def front_bank(f, job):
            return (f.part * NF + FRONT_AT[job]) % 2

        def front_turn(f, job):
            return f.half(NF, FRONT_AT[job])

        def slot_before(ck):
            if ck.part == 1:
                return 2
            return ck.turn % 2

        def slot_after(ck):
            return 2 if ck.part == 0 else 1

        def over_chunks(eng, front0, body, last):
            front0(Chunk(0, 0))
            for part in range(RATIO):
                body(Chunk(0, part), has_back=part > 0, has_front=True)
            with eng.Fori(1, TURNS - 1) as turn:
                for part in range(RATIO):
                    body(Chunk(turn, part), has_back=True, has_front=True)
            for part in range(RATIO):
                body(Chunk(TURNS - 1, part), has_back=True, has_front=part < RATIO - 1)
            last(Chunk(TURNS, 0))

        @block.sync
        def _(sp):
            loads = [
                (s_inp, in_proj_w.rearrange("(e p) m -> p e m", p=P)),
                (s_fc1, fc1_w.rearrange("(m p) i -> p m i", p=P)),
                (s_fc2, fc2_w.rearrange("(o p) m -> p o m", p=P)),
                (s_outp, out_proj_w.rearrange("(m p) d -> p m d", p=P)),
                (s_xp, x_proj_w),
                (s_dt, dt_proj_w.rearrange("(a p) r -> p a r", p=P)),
                (f1b[:], fc1_b.rearrange("(m p) -> p m", p=P)),
                (cw[:], conv_w.rearrange("(a p) w -> p a w", p=P)),
                (cb[:], conv_b.rearrange("(a p) -> p a", p=P)),
                (b_dt[:], dt_proj_b.rearrange("(a p) -> p a", p=P)),
                (d_col[:], D.rearrange("(a p) -> p a", p=P)),
                (A[:], A_log.rearrange("(a p) n -> p a n", p=P)),
                (w_gate[:], Wg.rearrange("(k p) e -> p k e", p=P)),
                (b_out[0:NE, :], be),
                (b_out[NE:NE + 1, :], fc2_b.rearrange("(a n) -> a n", a=1)),
            ]
            for k in range(KT):
                loads.append((w_exp[:, k, :].rearrange("p (e o) -> p e o", o=DM), We[:, k * P:(k + 1) * P, :].rearrange("e p o -> p e o")))
            for t in range(TB):
                loads.append((b_gate[:, t, :], bg.rearrange("(a n) -> a n", a=1).to_broadcast((P, NE))))
            assert len(loads) == N_LOADS

            def load(f):
                wait(sp, moe_added, f.count(2 * 16, -2 * 2 * 16 + 2 * TB))
                sp.dma_start(xin[:, f.part, :, :], x_v[f.index]).then_inc(x_loaded[f.part], 16)

            load(Chunk(0, 0))
            for dst, src in loads:
                sp.dma_start(dst, src, allow_slow_non_contiguous=True).then_inc(w_loaded, 16)

            def body(ck, has_back, has_front):
                if has_front:
                    load(ck.step(1))
                if has_back:
                    store(ck.step(-1))

            def store(b):
                wait(sp, out_ready, b.count(TB, TB))
                sp.dma_start(out_v[b.index], acc[:]).then_inc(out_stored, 16)

            over_chunks(sp, lambda f: None, body, lambda ck: store(ck.step(-1)))
            sp.wait_ge(out_stored, 16 * CHUNKS)

        @block.gpsimd
        def _(pool):
            pool.memset(ident[:], 0.0).then_inc(consts_set, 1)
            pool.memset(state[:], 0.0).then_inc(consts_set, 1)
            pool.memset(hist[:], 0.0).then_inc(consts_set, 1)
            pool.memset(half_neg[:], -0.5).then_inc(consts_set, 1)
            pool.memset(gates[:, :, :, NE:NE + 1], 1.0).then_inc(consts_set, 1)
            for e in range(NE):
                pool.memset(prio[:, :, e:e + 1], float(NE - e)).then_inc(consts_set, 1)
            pool.wait_ge(consts_set, 1)
            pool.affine_select(out=ident[:], in_=ident[:], compare_op=ALU.not_equal, fill=1.0, base=0,
                               pattern=[[-1, P]], channel_multiplier=1).then_inc(consts_set, 1)
            pool.wait_ge(consts_set, 6 + NE)
            pool.wait_ge(w_loaded, 16 * N_LOADS)
            for a in range(DT):
                for w in range(TAPS):
                    pool.tensor_scalar(w_conv[:, a, w, :], ident[:], cw[:, a, w:w + 1], 1.0,
                                       ALU.mult, ALU.mult).then_inc(consts_set, 1)
            pool.wait_ge(A_exp, 1)
            pool.tensor_scalar(A[:], A[:], -1.0, 1.0, ALU.mult, ALU.mult).then_inc(consts_set, 1)

            def norm(f):
                pool.wait_ge(ln_chain, f.count(N_LN, N_LN))
                wait(pool, norm_chain, f.count(N_NORM))
                apart(pool, passed)
                pool.tensor_scalar(rstd[:, 0, :], mv[:, :, 1], EPS, 1.0, ALU.add, ALU.mult).then_inc(norm_chain, 1)
                pool.tensor_scalar(rstd[:, 2, :], mv[:, :, 0], -1.0, 1.0, ALU.mult, ALU.mult).then_inc(norm_chain, 1)
                pool.wait_ge(norm_chain, f.count(N_NORM, 2))
                pool.tensor_tensor(rstd[:, 1, :], rstd[:, 0, :], half_neg[:], ALU.pow).then_inc(norm_chain, 1)
                pool.wait_ge(norm_chain, f.count(N_NORM, 3))
                pool.tensor_tensor(rstd[:, 0, :], rstd[:, 2, :], rstd[:, 1, :], ALU.mult).then_inc(norm_chain, 1)
                pool.wait_ge(norm_chain, f.count(N_NORM, 4))
                wait(pool, front_filled, f.count(NF, -NF + FRONT_AT[("conv", 3)] + 1))
                wait(pool, hist_saved, f.count(1))
                apart(pool, passed)
                for t in range(TB):
                    pool.tensor_scalar(xn[:, t, :], xin[:, f.part, t, :], rstd[:, 1, t:t + 1], rstd[:, 0, t:t + 1],
                                       ALU.mult, ALU.add).then_inc(norm_chain, 1)

            def clamp(f):
                pool.wait_ge(v_ready, f.count(DT, DT))
                wait(pool, dA_ready, f.count(STEPS, -STEPS))
                apart(pool, passed)
                pool.tensor_scalar(dt[:, f.part, :, :], wide[:], EXP_CAP, -BIG, ALU.min, ALU.max).then_inc(vmin_ready, 1)

            def times_u(f):
                pool.wait_ge(dt_ready, f.count(1, 1))
                pool.tensor_tensor(wide[:], dt[:, f.part, :, :], u[:, f.part, :, :], ALU.mult).then_inc(du_ready, 1)

            def gate_y(b, k):
                pool.wait_ge(yd_ready, b.count(DT, k + 1))
                pool.wait_ge(silu_ready, b.count(2, 2))
                pool.tensor_tensor(wide[:, k, :], wide[:, k, :], sz[:, b.part, k, :], ALU.mult).then_inc(yg_ready, 1)

            def scale_b(ck, n):
                if n == 0:
                    pool.wait_ge(duT_ready, ck.count(TB, TB))
                    pool.wait_ge(bc_ready, ck.count(1, 1))
                wait(pool, x_filled, ck.count(STEPS, DT * (n - 1)))
                apart(pool, passed)
                for t in range(TB):
                    ins = pool.tensor_scalar(xb[:, n % 2, t, :], duT[:, ck.part, t, :], bc[:, ck.part, t, R + n:R + n + 1],
                                             1.0, ALU.mult, ALU.mult)
                ins.then_inc(xb_ready, 1)

            def save_state(ck, n):
                wait(pool, scan_done, ck.count(STEPS, DT * (n + 1)))
                apart(pool, passed)
                pool.tensor_copy(state[:, slot_after(ck), n, :], h[:, n % 2, :, CT - 1]).then_inc(state_saved, 1)

            def steps(ck, has_back, has_front, has_steps=True):
                f, b = ck.step(1), ck.step(-1)
                for q in range(STEPS):
                    n = q // DT
                    if has_steps and q % DT == 0:
                        scale_b(ck, n)
                        if n > 0:
                            save_state(ck, n - 1)
                        elif not (ck.is_int() and ck.index == 0):
                            save_state(b, NSTATE - 1)
                    if has_front:
                        if q == Q_NORM:
                            norm(f)
                        if q == Q_MIN:
                            clamp(f)
                        if q == Q_DTU:
                            times_u(f)
                    if has_back:
                        for k in range(DT):
                            if q == Q_YG[k] + 2:
                                gate_y(b, k)

            over_chunks(pool, lambda f: steps(f.step(-1), False, True, False), steps,
                        lambda ck: steps(ck, True, False, False))

        @block.scalar
        def _(act):
            act.wait_ge(w_loaded, 16 * N_LOADS)
            act.activation(A[:], A[:], ACT.Exp).then_inc(A_exp, 1)
            for i, (_, dst, src) in enumerate(prep_jobs):
                act.wait_ge(prep_filled, i + 1)
                act.copy(dst, src(ps_x[i % 2])).then_inc(prep_copied, 1)

            def take(f, job):
                act.wait_ge(front_filled, f.count(NF, FRONT_AT[job] + 1))
                bank = front_bank(f, job)
                return ps_f[bank], front_freed[bank]

            def front(f, q):
                for k in range(KT):
                    if q == Q_XNT[k] + 2:
                        if k == 0:
                            wait(act, side_filled, f.step(-2).count(NS, NS - NB))
                        bank, freed = take(f, ("xnT", k))
                        act.copy(xnT[:, f.part, k, :], bank[:]).then_inc(xnT_ready, 1)
                        act.wait_ge(xnT_ready, f.count(KT, k + 1))
                        act.nop().then_inc(freed, 1)
                for k in range(DT):
                    if q == Q_XC[k] + 2:
                        bank, freed = take(f, ("xc", k))
                        act.activation(xc[:, k, HIST:], bank[:], ACT.Identity, bias=b_xz[:, k:k + 1]).then_inc(xc_ready, 1)
                        act.wait_ge(xc_ready, f.count(DT, k + 1))
                        act.nop().then_inc(freed, 1)
                    if q == Q_Z[k] + 2:
                        bank, freed = take(f, ("z", k))
                        if k == 0:
                            wait(act, yg_ready, f.count(DT, -DT))
                        act.activation(sz[:, f.part, k, :], bank[:], ACT.Identity,
                                       bias=b_xz[:, DT + k:DT + k + 1]).then_inc(pre_ready, 1)
                        act.wait_ge(pre_ready, f.count(2 * DT, k + 1))
                        act.nop().then_inc(freed, 1)
                    if q == Q_CONV[k] + 2:
                        bank, freed = take(f, ("conv", k))
                        if k == 0:
                            wait(act, yd_ready, f.count(DT, -DT))
                        act.activation(u[:, f.part, k, :], bank[:], ACT.Identity, bias=cb[:, k:k + 1]).then_inc(pre_ready, 1)
                        act.wait_ge(pre_ready, f.count(2 * DT, DT + k + 1))
                        act.nop().then_inc(freed, 1)
                if q == Q_SILU:
                    act.activation(u[:, f.part, :, :], u[:, f.part, :, :], ACT.Silu).then_inc(silu_ready, 1)
                    act.activation(sz[:, f.part, :, :], sz[:, f.part, :, :], ACT.Silu).then_inc(silu_ready, 1)
                if q == Q_LOGIT + 5:
                    act.wait_ge(top_ready, f.count(1, 1))
                    act.activation(gs[:, 4, :], gs[:, 3, :], ACT.Exp).then_inc(e2_ready, 1)
                if q == Q_XD + 1:
                    bank, freed = take(f, ("xd", 0))
                    act.copy(xdT[:], bank[0:XD, :]).then_inc(xd_ready, 1)
                    act.wait_ge(xd_ready, f.count(1, 1))
                    act.nop().then_inc(freed, 1)
                if q == Q_BC + 1:
                    bank, freed = take(f, ("bc", 0))
                    wait(act, y_added, f.count(STEPS, -STEPS))
                    act.copy(bc[:, f.part, :, :], bank[:, 0:TB * XD].rearrange("p (t x) -> p t x", t=TB)).then_inc(bc_ready, 1)
                    act.wait_ge(bc_ready, f.count(1, 1))
                    act.nop().then_inc(freed, 1)
                if q == Q_SP:
                    act.wait_ge(vmin_ready, f.count(1, 1))
                    act.activation(dt[:, f.part, :, :], dt[:, f.part, :, :], ACT.Exp).then_inc(sp_chain, 1)
                    act.wait_ge(sp_chain, f.count(2, 1))
                    act.activation(dt[:, f.part, :, :], dt[:, f.part, :, :], ACT.Ln, bias=1.0).then_inc(sp_chain, 1)
                for k in range(TB):
                    if q == Q_DUT[k] + 1:
                        bank, freed = take(f, ("duT", k))
                        if k == 0:
                            wait(act, xb_ready, f.count(NSTATE, -NSTATE))
                        act.copy(duT[:, f.part, k, :], bank[:]).then_inc(duT_ready, 1)
                        act.wait_ge(duT_ready, f.count(TB, k + 1))
                        act.nop().then_inc(freed, 1)

            def decay(ck, q):
                n, k = q // DT, q % DT
                if q == 0:
                    act.wait_ge(dt_ready, ck.count(1, 1))
                wait(act, scan_done, ck.count(STEPS, q - DT + 1))
                act.activation(dA[:, k, :], dt[:, ck.part, k, :], ACT.Exp, scale=A[:, k, n:n + 1]).then_inc(dA_ready, 1)

            def steps(ck, has_back, has_front, has_steps=True):
                f, b = ck.step(1), ck.step(-1)
                for q in range(STEPS):
                    if has_steps:
                        decay(ck, q)
                    if has_front:
                        front(f, q)
                    if has_back and q == Q_GT + 1:
                        act.wait_ge(side_filled, side_count(ck, ("gT", 0), 1))
                        act.copy(gT[:], ps_s[side_bank(ck, ("gT", 0))][0:NE + 1, :]).then_inc(gT_ready, 1)
                        act.wait_ge(gT_ready, b.count(1, 1))
                        act.nop().then_inc(side_freed[side_bank(ck, ("gT", 0))], 1)

            act.wait_ge(consts_set, N_CONSTS)
            over_chunks(act, lambda f: steps(f.step(-1), False, True, False), steps,
                        lambda ck: steps(ck, True, False, False))

        @block.vector
        def _(dve):
            def stats(f):
                dve.wait_ge(x_loaded[f.part], f.turn * 16 + 16)
                wait(dve, norm_chain, f.count(N_NORM))
                for t in range(TB):
                    dve.bn_stats(stat[:, t, :], xin[:, f.part, t, :]).then_inc(ln_chain, 1)
                dve.wait_ge(ln_chain, f.count(N_LN, TB))
                apart(dve, passed)
                for t in range(TB):
                    dve.bn_aggr(mv[:, t, :], stat[:, t, :]).then_inc(ln_chain, 1)

            def top2(f, first):
                n = [0 if first else 13]

                def link(ins):
                    ins.then_inc(gate_chain, 1)
                    n[0] += 1
                    dve.wait_ge(gate_chain, f.count(N_GATE, n[0]))

                def wide_of(col):
                    return gs[:, col, :].unsqueeze(2).to_broadcast([P, TB, NE])

                lg, eq, r, k1, l2, k2 = (gw[:, i, :, :] for i in range(6))
                if first:
                    bank = front_bank(f, ("logit", 0))
                    dve.wait_ge(front_filled, f.count(NF, FRONT_AT[("logit", 0)] + 1))
                    link(dve.tensor_tensor(lg, ps_f[bank][:, 0:TB * NE].rearrange("p (t e) -> p t e", t=TB), b_gate[:], ALU.add))
                    dve.nop().then_inc(front_freed[bank], 1)
                    link(dve.tensor_reduce(gs[:, 0, :], lg, AX_X, ALU.max))
                    link(dve.tensor_tensor(eq, lg, wide_of(0), ALU.is_equal))
                    link(dve.tensor_tensor(r, eq, prio[:], ALU.mult))
                    link(dve.tensor_reduce(gs[:, 1, :], r, AX_X, ALU.max))
                    link(dve.tensor_tensor(k1, r, wide_of(1), ALU.is_equal))
                    link(dve.scalar_tensor_tensor(l2, k1, -BIG, lg, ALU.mult, ALU.add))
                    link(dve.tensor_reduce(gs[:, 2, :], l2, AX_X, ALU.max))
                    link(dve.tensor_tensor(eq, l2, wide_of(2), ALU.is_equal))
                    link(dve.tensor_tensor(r, eq, prio[:], ALU.mult))
                    link(dve.tensor_reduce(gs[:, 1, :], r, AX_X, ALU.max))
                    link(dve.tensor_tensor(k2, r, wide_of(1), ALU.is_equal))
                    wait(dve, e2_ready, f.count(1))
                    link(dve.tensor_tensor(gs[:, 3, :], gs[:, 2, :], gs[:, 0, :], ALU.subtract))
                    dve.nop().then_inc(top_ready, 1)
                else:
                    dve.wait_ge(e2_ready, f.count(1, 1))
                    link(dve.tensor_scalar(gs[:, 5, :], gs[:, 4, :], 1.0, None, ALU.add))
                    link(dve.reciprocal(gs[:, 6, :], gs[:, 5, :]))
                    link(dve.tensor_tensor(gs[:, 7, :], gs[:, 4, :], gs[:, 6, :], ALU.mult))
                    dve.tensor_tensor(eq, k1, wide_of(6), ALU.mult)
                    link(dve.tensor_tensor(r, k2, wide_of(7), ALU.mult))
                    wait(dve, gT_ready, f.count(1, -1))
                    dve.tensor_tensor(gates[:, f.part, :, 0:NE], eq, r, ALU.add).then_inc(gates_ready, 1)

            def front(f, q):
                if q == Q_STATS:
                    stats(f)
                if q == Q_LOGIT + 2:
                    top2(f, True)
                if q == Q_LOGIT + 6:
                    top2(f, False)
                if q == Q_XNT[1] + 1:
                    dve.wait_ge(front_filled, f.count(NF, FRONT_AT[("xnT", KT - 1)] + 1))
                    wait(dve, hist_saved, f.count(1))
                    dve.tensor_copy(xc[:, :, 0:HIST], hist[:, slot_before(f), :, :]).then_inc(hist_set, 1)
                if q == Q_XC[-1] + 4:
                    dve.wait_ge(xc_ready, f.count(DT, DT))
                    dve.tensor_copy(hist[:, slot_after(f), :, :], xc[:, :, CT:CT + HIST]).then_inc(hist_saved, 1)
                for k in range(DT):
                    if q == Q_DT[k] + 1:
                        bank = front_bank(f, ("dt", k))
                        dve.wait_ge(front_filled, f.count(NF, FRONT_AT[("dt", k)] + 1))
                        dve.tensor_scalar(wide[:, k, :], ps_f[bank][:], b_dt[:, k:k + 1], None, ALU.add).then_inc(v_ready, 1)
                        dve.wait_ge(v_ready, f.count(DT, k + 1))
                        dve.nop().then_inc(front_freed[bank], 1)
                if q == Q_MAX:
                    dve.wait_ge(sp_chain, f.count(2, 2))
                    dve.tensor_tensor(dt[:, f.part, :, :], dt[:, f.part, :, :], wide[:], ALU.max).then_inc(dt_ready, 1)

            def back(ck, q):
                b = ck.step(-1)
                for k in range(DT):
                    if q == Q_YG[k] + 1:
                        job = ("yg", k)
                        dve.wait_ge(side_filled, side_count(ck, job, 1))
                        dve.scalar_tensor_tensor(wide[:, k, :], u[:, b.part, k, :], d_col[:, k:k + 1], ps_s[side_bank(ck, job)][:],
                                                 ALU.mult, ALU.add).then_inc(yd_ready, 1)
                        dve.wait_ge(yd_ready, b.count(DT, k + 1))
                        dve.nop().then_inc(side_freed[side_bank(ck, job)], 1)
                for t in range(TB):
                    if q == Q_OUT[t] + 1:
                        job = ("out", t)
                        dve.wait_ge(side_filled, side_count(ck, job, 1))
                        dve.wait_ge(moe_added, b.count(2 * 16, 2 * 16))
                        dve.tensor_tensor(acc[:, t, :], ps_s[side_bank(ck, job)][:, 0:DM], acc[:, t, :], ALU.add).then_inc(out_ready, 1)
                        dve.wait_ge(out_ready, b.count(TB, t + 1))
                        dve.nop().then_inc(side_freed[side_bank(ck, job)], 1)

            def experts(ck, q):
                for i in range(16):
                    if q == Q_MOE[i] + 1:
                        pair, t = i // TB, i % TB
                        job = ("moe", i)
                        bank = side_bank(ck, job)
                        if i == 0:
                            wait(dve, out_stored, ck.count(16))
                            dve.wait_ge(gates_ready, ck.count(1, 1))
                        dve.wait_ge(side_filled, side_count(ck, job, 1))
                        for j in range(2):
                            e = 2 * pair + j
                            if e > 0:
                                dve.wait_ge(moe_added, ck.count(2 * 16, 2 * i + 1 if j else 2 * (i - TB) + 2))
                            dve.scalar_tensor_tensor(acc[:, t, :], ps_s[bank][:, j * DM:(j + 1) * DM],
                                                     gates[:, ck.part, t, e:e + 1],
                                                     xin[:, ck.part, t, :] if e == 0 else acc[:, t, :],
                                                     ALU.mult, ALU.add).then_inc(moe_added, 1)
                        dve.wait_ge(moe_added, ck.count(2 * 16, 2 * i + 2))
                        dve.nop().then_inc(side_freed[bank], 1)

            def scan(ck, q):
                n, k = q // DT, q % DT
                if k == 0:
                    wait(dve, h_filled, ck.count(STEPS, DT * (n - 1)))
                    wait(dve, state_saved, ck.count(NSTATE, n - 1))
                dve.wait_ge(dA_ready, ck.count(STEPS, q + 1))
                dve.wait_ge(x_filled, ck.count(STEPS, q + 1))
                dve.tensor_tensor_scan(h[:, n % 2, k, :], dA[:, k, :], ps_x[q % 2][:],
                                       state[:, slot_before(ck), n, k:k + 1], ALU.mult, ALU.add).then_inc(scan_done, 1)

            def add_y(ck, n, t):
                i = DT * n + t
                dve.wait_ge(h_filled, ck.count(STEPS, i + 1))
                if n == 0:
                    if t == 0:
                        dve.wait_ge(bc_ready, ck.count(1, 1))
                        wait(dve, side_filled, side_count(ck.step(-1), ("yg", DT - 1), 1))
                    dve.tensor_scalar(yT[:, ck.part, t, :], ps_h[t % 2][:], bc[:, ck.part, t, R + NSTATE:R + NSTATE + 1],
                                      None, ALU.mult).then_inc(y_added, 1)
                else:
                    dve.wait_ge(y_added, ck.count(STEPS, i - TB + 1))
                    dve.scalar_tensor_tensor(yT[:, ck.part, t, :], ps_h[t % 2][:],
                                             bc[:, ck.part, t, R + NSTATE + n:R + NSTATE + n + 1],
                                             yT[:, ck.part, t, :], ALU.mult, ALU.add).then_inc(y_added, 1)

            def steps(ck, has_back, has_front, has_steps=True):
                f, b = ck.step(1), ck.step(-1)
                for q in range(STEPS):
                    if has_steps:
                        scan(ck, q)
                    if q >= DT:
                        if has_steps:
                            add_y(ck, q // DT - 1, q % DT)
                    elif has_back or (has_steps and not (ck.is_int() and ck.index == 0)):
                        add_y(b, NSTATE - 1, q)
                    if has_front:
                        front(f, q)
                    if has_back:
                        back(ck, q)
                    if has_steps:
                        experts(ck, q)

            dve.wait_ge(w_loaded, 16 * N_LOADS)
            dve.wait_ge(consts_set, N_CONSTS)
            over_chunks(dve, lambda f: steps(f.step(-1), False, True, False), steps,
                        lambda ck: steps(ck, True, False, False))

        @block.tensor
        def _(pe):
            pe.wait_ge(w_loaded, 16 * N_LOADS)
            pe.wait_ge(consts_set, N_CONSTS)
            for i, (fill, _, _) in enumerate(prep_jobs):
                wait(pe, prep_copied, i - 1)
                last = fill(pe, ps_x[i % 2])
                last.then_inc(prep_filled, 1)
            pe.wait_ge(prep_copied, len(prep_jobs))

            def mm(out, lhsT, rhs, k, n):
                return pe.matmul(out, lhsT, rhs, start=k == 0, stop=k == n - 1)

            def fill_front(f, job):
                kind, k = job
                bank = ps_f[front_bank(f, job)]
                wait(pe, front_freed[front_bank(f, job)], front_turn(f, job))
                if kind == "xnT":
                    pe.wait_ge(norm_chain, f.count(N_NORM, N_NORM))
                    for t in range(TB):
                        last = pe.transpose(bank[:, t * P:(t + 1) * P], xn[:, t, k * P:(k + 1) * P], ident[:])
                elif kind == "logit":
                    pe.wait_ge(xnT_ready, f.count(KT, KT))
                    for t in range(TB):
                        for i in range(KT):
                            last = mm(bank[:, t * NE:(t + 1) * NE], xnT[:, f.part, i, t * P:(t + 1) * P], w_gate[:, i, :], i, KT)
                elif kind in ("xc", "z"):
                    e = k + (DT if kind == "z" else 0)
                    for i in range(KT):
                        last = mm(bank[:], w_xz[:, i, e * P:(e + 1) * P], xnT[:, f.part, i, :], i, KT)
                elif kind == "conv":
                    pe.wait_ge(xc_ready, f.count(DT, k + 1))
                    pe.wait_ge(hist_set, f.count(1, 1))
                    for w in range(TAPS):
                        last = mm(bank[:], w_conv[:, k, w, :], xc[:, k, w:w + CT], w, TAPS)
                elif kind == "xd":
                    pe.wait_ge(silu_ready, f.count(2, 1))
                    for i in range(DT):
                        last = mm(bank[0:XD, :], w_xd[:, i, :], u[:, f.part, i, :], i, DT)
                elif kind == "bc":
                    pe.wait_ge(xd_ready, f.count(1, 1))
                    apart(pe, passed)
                    for t in range(TB):
                        last = pe.transpose(bank[:, t * XD:(t + 1) * XD], xdT[:, t * P:(t + 1) * P], ident[0:XD, 0:XD])
                elif kind == "dt":
                    last = mm(bank[:], w_dt[:, k * P:(k + 1) * P], xdT[0:R, :], 0, 1)
                else:
                    pe.wait_ge(du_ready, f.count(1, 1))
                    for i in range(DT):
                        last = pe.transpose(bank[:, i * P:(i + 1) * P], wide[:, i, k * P:(k + 1) * P], ident[:])
                last.then_inc(front_filled, 1)

            def fill_side(ck, job):
                kind, k = job
                b = ck.step(-1)
                bank = ps_s[side_bank(ck, job)]
                wait(pe, side_freed[side_bank(ck, job)], side_turn(ck, job))
                if kind == "gT":
                    pe.wait_ge(gates_ready, b.count(1, 1))
                    for t in range(TB):
                        last = pe.transpose(bank[0:NE + 1, t * P:(t + 1) * P], gates[:, b.part, t, :], ident[:])
                elif kind == "yg":
                    pe.wait_ge(y_added, b.count(STEPS, STEPS))
                    for t in range(TB):
                        last = pe.transpose(bank[:, t * P:(t + 1) * P], yT[:, b.part, t, k * P:(k + 1) * P], ident[:])
                elif kind == "out":
                    pe.wait_ge(yg_ready, b.count(DT, DT))
                    pe.wait_ge(gT_ready, b.count(1, 1))
                    for i in range(DT):
                        mm(bank[:, 0:DM], wide[:, i, k * P:(k + 1) * P], w_out[:, i, :], i, DT + 1)
                    last = mm(bank[:, 0:DM], gT[:, k * P:(k + 1) * P], b_out[:], DT, DT + 1)
                else:
                    pair, t = k // TB, k % TB
                    for i in range(KT):
                        last = mm(bank[:], xnT[:, ck.part, i, t * P:(t + 1) * P], w_exp[:, i, pair * 2 * DM:(pair + 1) * 2 * DM], i, KT)
                last.then_inc(side_filled, 1)

            places_f = dict(zip(FRONT, (*Q_XNT, Q_LOGIT, *Q_XC, *Q_Z, *Q_CONV, Q_XD, Q_BC, *Q_DT, *Q_DUT)))
            places_s = dict(zip(SIDE, (Q_GT, *Q_YG, *Q_OUT, *Q_MOE)))

            def turn_x(ck, q):
                n, k = q // DT, q % DT
                if k == 0:
                    pe.wait_ge(xb_ready, ck.count(NSTATE, n + 1))
                wait(pe, scan_done, ck.count(STEPS, q - 1))
                for t in range(TB):
                    last = pe.transpose(ps_x[q % 2][:, t * P:(t + 1) * P], xb[:, n % 2, t, k * P:(k + 1) * P], ident[:])
                last.then_inc(x_filled, 1)

            def turn_h(ck, n, t):
                i = DT * n + t
                if t == 0:
                    pe.wait_ge(scan_done, ck.count(STEPS, DT * (n + 1)))
                wait(pe, y_added, ck.count(STEPS, i - 1))
                for k in range(DT):
                    last = pe.transpose(ps_h[t % 2][:, k * P:(k + 1) * P], h[:, n % 2, k, t * P:(t + 1) * P], ident[:])
                last.then_inc(h_filled, 1)

            def steps(ck, has_back, has_front, has_steps=True):
                f, b = ck.step(1), ck.step(-1)
                for q in range(STEPS):
                    if has_steps:
                        turn_x(ck, q)
                    if q >= DT:
                        if has_steps:
                            turn_h(ck, q // DT - 1, q % DT)
                    elif has_back or (has_steps and not (ck.is_int() and ck.index == 0)):
                        turn_h(b, NSTATE - 1, q)
                    if has_front:
                        for job in FRONT:
                            if places_f[job] == q:
                                fill_front(f, job)
                    for job in SIDE:
                        if places_s[job] == q and (has_back if job in BACK else has_steps):
                            fill_side(ck, job)

            over_chunks(pe, lambda f: steps(f.step(-1), False, True, False), steps,
                        lambda ck: steps(ck, True, False, False))


_INS = ['x', 'fc1_w', 'fc1_b', 'in_proj_w', 'conv_w', 'conv_b', 'x_proj_w', 'dt_proj_w', 'dt_proj_b',
        'A_log', 'D', 'out_proj_w', 'fc2_w', 'fc2_b']
_INS = ['L0_attn_' + n for n in _INS] + ['L0_ffn_We', 'L0_ffn_be', 'L0_ffn_Wg', 'L0_ffn_bg']


def kernel(**inputs):
    import numpy as _np
    import concourse.bacc as _bacc
    from concourse import mybir as _mybir
    from concourse.bass_utils import run_bass_kernel_spmd as _run

    nc = _bacc.Bacc("TRN2", target_bir_lowering=False, num_devices=1)
    arrays, args = {}, []
    for name in _INS:
        a = _np.ascontiguousarray(inputs[name])
        arrays[f"in_{name}_dram"] = a
        args.append(nc.dram_tensor(f"in_{name}_dram", a.shape, _mybir.dt.from_np(a.dtype), kind="ExternalInput").ap())
    shape = inputs['L0_attn_x'].shape
    args.append(nc.dram_tensor("out_0_dram", shape, _mybir.dt.float32, kind="ExternalOutput").ap())
    mamba_moe_kernel(nc, *args)
    r = _run(nc, [arrays], core_ids=[0])
    return r.results[0]["out_0_dram"]
```

```python
import concourse.bass as bass
from concourse import mybir
from contextlib import ExitStack

P = 128
F32 = mybir.dt.float32
F32R = mybir.dt.float32r
ALU = mybir.AluOpType
ACT = mybir.ActivationFunctionType
AX_X = mybir.AxisListType.X

EPS = 1e-5
BIG = 3.0e38
EXP_CAP = 40.0
RATIO = 2

Q_STATS = (0, 0, 1, 1)
Q_AGGR = 2
Q_NORM = 3
Q_GT = 1
Q_YG = (2, 3, 4, 5)
Q_XNT = (8, 9)
Q_XC = (10, 12, 15, 19)
Q_LOGIT = 13
Q_OUT = ((6, 7), (10, 11), (13, 14), (16, 17))
Q_CONV = (13, 16, 20, 24)
Q_TOP2 = tuple(range(15, 28))
Q_E2 = 28
Q_SHARE = (31, 32, 33, 34, 35, 36)
Q_Z = (20, 21, 23, 25)
Q_SILU = 29
Q_XD = (32, 33, 34, 36)
Q_BC = 37
Q_DT = (38, 39, 40, 41)
Q_MIN = (42, 43, 44, 45)
Q_SP = 47
Q_MAX = (50, 51, 52, 53)
Q_DTU = (51, 52, 53, 54)
Q_DUT = (56, 57, 58, 59)
Q_XB0 = 62
Q_MOE = (22, 24, 26, 28, 30, 35, 42, 43, 45, 47, 49, 51, 53, 55, 60, 61)

FRONT = ([("xnT", k) for k in range(2)] + [("xc", k) for k in range(2)] + [("logit", 0)] + [("xc", k) for k in (2, 3)]
         + [("xd", 0), ("bc", 0)]
         + [("dt", k) for k in range(4)] + [("duT", k) for k in range(4)])
BACK = [("gT", 0)] + [("yg", k) for k in range(4)] + [("out", k) for k in range(4)]
SIDE = BACK + [job for _, job in sorted([(q, ("z", k)) for k, q in enumerate(Q_Z)] + [(q, ("moe", k)) for k, q in enumerate(Q_MOE)])]
NF, NB, NS = len(FRONT), len(BACK), len(SIDE)
FRONT_AT = {job: i for i, job in enumerate(FRONT)}
SIDE_AT = {job: i for i, job in enumerate(SIDE)}


class Chunk:

    def __init__(self, turn, part):
        self.turn, self.part = turn, part
        self.index = turn * RATIO + part

    def count(self, per, more=0):
        return self.turn * (RATIO * per) + (self.part * per + more)

    def step(self, by):
        part = self.part + by
        return Chunk(self.turn + part // RATIO, part % RATIO)

    def is_int(self):
        return isinstance(self.turn, int)


def wait(eng, sem, value):
    if isinstance(value, int) and value <= 0:
        return
    eng.wait_ge(sem, value)


def apart(eng, passed):
    eng.nop().then_inc(passed, 1)


def mamba_moe_kernel(nc, x, fc1_w, fc1_b, in_proj_w, conv_w, conv_b, x_proj_w, dt_proj_w, dt_proj_b,
                     A_log, D, out_proj_w, fc2_w, fc2_b, We, be, Wg, bg, out):
    B, L, DM = x.shape
    DI, NSTATE = A_log.shape
    TAPS = conv_w.shape[1]
    R = dt_proj_w.shape[1]
    XD = R + 2 * NSTATE
    NE = Wg.shape[1]
    KT, DT, ET = DM // P, DI // P, 2 * DI // P
    CT = 512
    TB = CT // P
    CHUNKS = B * L // CT
    PER_BATCH = L // CT
    STEPS = NSTATE * DT
    HIST = TAPS - 1
    G0 = 64
    assert DM == 256 and DI == 512 and TB == DT == 4 and PER_BATCH == 2 * RATIO and CHUNKS % RATIO == 0
    TURNS = CHUNKS // RATIO

    x_v = x.rearrange("b (c t p) d -> (b c) p t d", t=TB, p=P)
    out_v = out.rearrange("b (c t p) d -> (b c) p t d", t=TB, p=P)

    with ExitStack() as ctx:
        def sb(name, shape, dtype=F32):
            return ctx.enter_context(nc.sbuf_tensor(name, shape, dtype))

        def sem(name):
            return ctx.enter_context(nc.semaphore(name))

        ident = sb("ident", [P, P])
        w_xz = sb("w_xz", [P, 2, KT, 2 * DI], F32R)
        b_xz = sb("b_xz", [P, ET])
        w_xd = sb("w_xd", [P, DT, XD])
        w_dt = sb("w_dt", [R, DI])
        w_out = sb("w_out", [P, DT, DM])
        w_exp = sb("w_exp", [P, 2, KT, NE * DM], F32R)
        b_out = sb("b_out", [P, DM])[G0:G0 + NE + 1, :]
        w_gate = sb("w_gate", [P, 2, KT, NE], F32R)
        b_gate = sb("b_gate", [P, TB, NE])
        prio = sb("prio", [P, TB, NE])
        cw = sb("cw", [P, DT, TAPS])
        cb = sb("cb", [P, DT])
        b_dt = sb("b_dt", [P, DT])
        d_col = sb("d_col", [P, DT])
        f1b = sb("f1b", [P, KT])
        A = sb("A", [P, DT, NSTATE])
        half_neg = sb("half_neg", [P, TB])
        ones = sb("ones", [P, 1])
        ln_probe = sb("ln_probe", [P, 1])

        xin = sb("xin", [P, 2, TB, DM])
        xc = sb("xc", [P, 2, HIST + CT])
        xn = xc[:].rearrange("p a b -> p (a b)")[:, 0:TB * DM].rearrange("p (t d) -> p t d", t=TB)
        xnT = sb("xnT", [P, 2, 2, KT, CT], F32R)
        u = sb("u", [P, 2, DT, CT])
        sz = sb("sz", [P, DT, CT])
        dt = sb("dt", [P, 2, DT, CT])
        wide = sb("wide", [P, DT, CT])
        duT = sb("duT", [P, 2, TB, DI])
        bc = sb("bc", [P, 2, TB, XD])
        small = sb("small", [P, CT])
        xdT = small[0:XD, :]
        gates = sb("gates", [P, 2, TB, NE + 1])
        gT = small[G0:G0 + NE + 1, :]
        acc = sb("acc", [P, TB, DM])
        stat = sb("stat", [P, TB, 6])
        mv = sb("mv", [P, TB, 2])
        rstd = sb("rstd", [P, 3, TB])
        gw = sb("gw", [P, 8, TB, NE])
        gs = sb("gs", [P, 8, TB])
        hist = sb("hist", [P, 3, DT, HIST])
        state = sb("state", [P, 3, NSTATE, DT])
        xb = sb("xb", [P, 2, TB, DI])
        dA = sb("dA", [P, DT, CT])
        h = sb("h", [P, 2, DT, CT])
        yT = sb("yT", [P, TB, DI])

        s_inp = xb[:, 0, :, :].rearrange("p a b -> p (a b)")[:, 0:ET * DM].rearrange("p (e m) -> p e m", m=DM)
        s_fc1 = xb[:, 1, 0, :].rearrange("p (m i) -> p m i", m=KT)
        s_fc2 = xb[:, 1, 1, :].rearrange("p (o m) -> p o m", o=KT)
        s_outp = xb[:, 1, 2:4, :]
        s_xp = dA[0:XD, 0, :]
        s_dt = dA[:, 1, 0:DT * R].rearrange("p (a r) -> p a r", a=DT)
        s_inT = h[:, 0, :, :].rearrange("p a b -> p (a b)").rearrange("p (m e) -> p m e", m=KT)
        s_exp = [yT[:].rearrange("p a b -> p (a b)"), u[:, 0, :, :].rearrange("p a b -> p (a b)")]
        s_gate = dA[:, 2, 0:KT * NE].rearrange("p (k e) -> p k e", e=NE)
        s_fc2T = h[:, 1, 0, :].rearrange("p (m o) -> p m o", m=KT)

        def psum(name):
            return ctx.enter_context(nc.psum_tensor(name, [P, 512], F32))

        ps_x = [psum(f"ps_x{i}") for i in range(2)]
        ps_h = [psum(f"ps_h{i}") for i in range(2)]
        ps_f = [psum(f"ps_f{i}") for i in range(2)]
        ps_s = [psum(f"ps_s{i}") for i in range(2)]

        passed = sem("passed")
        w_loaded = sem("w_loaded")
        consts_set = sem("consts_set")
        A_exp = sem("A_exp")
        prep_filled = sem("prep_filled")
        prep_copied = sem("prep_copied")
        prep_split = sem("prep_split")
        x_loaded = [sem(f"x_loaded{i}") for i in range(RATIO)]
        out_stored = sem("out_stored")
        ln_chain = sem("ln_chain")
        norm_chain = sem("norm_chain")
        gate_chain = sem("gate_chain")
        e2_ready = sem("e2_ready")
        front_filled = sem("front_filled")
        side_filled = sem("side_filled")
        xnT_ready = sem("xnT_ready")
        hist_set = sem("hist_set")
        hist_saved = sem("hist_saved")
        xc_ready = sem("xc_ready")
        z_ready = sem("z_ready")
        taps_ready = sem("taps_ready")
        conv_chain = sem("conv_chain")
        xnL_ready = sem("xnL_ready")
        split_done = sem("split_done")
        u_ready = sem("u_ready")
        sz_ready = sem("sz_ready")
        probed = sem("probed")
        xd_ready = sem("xd_ready")
        bc_ready = sem("bc_ready")
        v_ready = sem("v_ready")
        vmin_ready = sem("vmin_ready")
        sp_chain = sem("sp_chain")
        dt_ready = sem("dt_ready")
        du_ready = sem("du_ready")
        duT_ready = sem("duT_ready")
        xb_ready = sem("xb_ready")
        x_filled = sem("x_filled")
        dA_ready = sem("dA_ready")
        scan_done = sem("scan_done")
        state_saved = sem("state_saved")
        h_filled = sem("h_filled")
        y_added = sem("y_added")
        gT_ready = sem("gT_ready")
        yd_ready = sem("yd_ready")
        yg_ready = sem("yg_ready")
        moe_first = sem("moe_first")
        moe_second = sem("moe_second")
        out_ready = sem("out_ready")

        N_LOADS = 15 + KT + TB
        N_CONSTS = 6 + NE + 1 + 1

        def turn_in(m, half):
            def fill(pe, bank):
                for i in range(4):
                    last = pe.transpose(bank[:, i * P:(i + 1) * P], s_inp[:, 4 * half + i, m * P:(m + 1) * P], ident[:])
                return last
            return fill, s_inT[:, m, half * 512:(half + 1) * 512], lambda bank: bank[:]

        def turn_fc2(m):
            def fill(pe, bank):
                for o in range(KT):
                    last = pe.transpose(bank[:, o * P:(o + 1) * P], s_fc2[:, o, m * P:(m + 1) * P], ident[:])
                return last
            return fill, s_fc2T[:, m, :], lambda bank: bank[:, 0:DM]

        def turn_xd(pe, bank):
            for i in range(DT):
                last = pe.transpose(bank[:, i * XD:(i + 1) * XD], s_xp[:, i * P:(i + 1) * P], ident[0:XD, 0:XD])
            return last

        def turn_dt(pe, bank):
            for i in range(DT):
                last = pe.transpose(bank[0:R, i * P:(i + 1) * P], s_dt[:, i, :], ident[:])
            return last

        def join_in(i, half):
            def fill(pe, bank):
                pe.wait_ge(prep_copied, 4)
                for m in range(KT):
                    last = pe.matmul(bank[:], s_fc1[:, m, i * P:(i + 1) * P], s_inT[:, m, half * 512:(half + 1) * 512],
                                     start=m == 0, stop=m == KT - 1)
                return last
            return fill, w_xz[:, 0, i, half * 512:(half + 1) * 512], lambda bank: bank[:]

        def join_bias(pe, bank):
            for e in range(ET):
                for m in range(KT):
                    last = pe.matmul(bank[:, e:e + 1], s_inT[:, m, e * P:(e + 1) * P], f1b[:, m:m + 1],
                                     start=m == 0, stop=m == KT - 1)
            return last

        def join_out(a):
            def fill(pe, bank):
                pe.wait_ge(prep_copied, 6)
                for m in range(KT):
                    last = pe.matmul(bank[:, 0:DM], s_outp[:, m, a * P:(a + 1) * P], s_fc2T[:, m, :],
                                     start=m == 0, stop=m == KT - 1)
                return last
            return fill, w_out[:, a, :], lambda bank: bank[:, 0:DM]

        N_SPLIT = 1 + KT + 1 + KT
        JOIN_AT = 2 * KT + KT + 2

        prep_jobs = ([turn_in(m, half) for m in range(KT) for half in range(2)] + [turn_fc2(m) for m in range(KT)]
                     + [(turn_xd, w_xd[:], lambda bank: bank[:, 0:DT * XD].rearrange("p (a x) -> p a x", a=DT)),
                        (turn_dt, w_dt[:], lambda bank: bank[0:R, :])]
                     + [join_in(i, half) for i in range(KT) for half in range(2)]
                     + [(join_bias, b_xz[:], lambda bank: bank[:, 0:ET])] + [join_out(a) for a in range(DT)])

        block = ctx.enter_context(nc.Block())

        N_LN = 2 * TB
        N_TAP = DT * (TAPS - 1)
        N_CONV = DT * TAPS
        N_NORM = 4 + TB
        N_GATE = len(Q_TOP2) + len(Q_SHARE)

        def side_count(ck, job, more=0):
            return ck.count(NS, SIDE_AT[job] - NB + more)

        def side_bank(ck, job):
            return (ck.part * NS + SIDE_AT[job] - NB) % 2

        def front_bank(f, job):
            return (f.part * NF + FRONT_AT[job]) % 2

        def front_taken(f, job):
            kind, k = job
            return {
                "xnT": (xnL_ready, f.count(KT, k + 1)), "xc": (xc_ready, f.count(DT, k + 1)),
                "logit": (gate_chain, f.count(N_GATE, 1)), "xd": (xd_ready, f.count(1, 1)),
                "bc": (bc_ready, f.count(1, 1)), "dt": (v_ready, f.count(DT, k + 1)),
                "duT": (duT_ready, f.count(TB, k + 1)),
            }[kind]

        def side_taken(ck, job):
            kind, k = job
            b = ck.step(-1)
            return {
                "gT": (gT_ready, b.count(1, 1)), "yg": (yd_ready, b.count(DT * TB, DT * (k + 1))),
                "out": (out_ready, b.count(TB, k + 1)), "z": (z_ready, ck.count(DT, k + 1)),
                "moe": (moe_second, ck.count(16, k + 1)),
            }[kind]

        def two_before(ck, job, order, at):
            i = at[job] - 2
            return (ck, order[i]) if i >= 0 else (ck.step(-1), order[i + len(order)])

        def slot_before(ck):
            if ck.part == 1:
                return 2
            return ck.turn % 2

        def slot_after(ck):
            return 2 if ck.part == 0 else 1

        def over_chunks(eng, front0, body, last):
            front0(Chunk(0, 0))
            for part in range(RATIO):
                body(Chunk(0, part), has_back=part > 0, has_front=True)
            with eng.Fori(1, TURNS - 1) as turn:
                for part in range(RATIO):
                    body(Chunk(turn, part), has_back=True, has_front=True)
            for part in range(RATIO):
                body(Chunk(TURNS - 1, part), has_back=True, has_front=part < RATIO - 1)
            last(Chunk(TURNS, 0))

        @block.sync
        def _(sp):
            loads = [
                (s_inp, in_proj_w.rearrange("(e p) m -> p e m", p=P)),
                (s_fc1, fc1_w.rearrange("(m p) i -> p m i", p=P)),
                (s_fc2, fc2_w.rearrange("(o p) m -> p o m", p=P)),
                (s_outp, out_proj_w.rearrange("(m p) d -> p m d", p=P)),
                (s_xp, x_proj_w),
                (s_dt, dt_proj_w.rearrange("(a p) r -> p a r", p=P)),
                (f1b[:], fc1_b.rearrange("(m p) -> p m", p=P)),
                (cw[:], conv_w.rearrange("(a p) w -> p a w", p=P)),
                (cb[:], conv_b.rearrange("(a p) -> p a", p=P)),
                (b_dt[:], dt_proj_b.rearrange("(a p) -> p a", p=P)),
                (d_col[:], D.rearrange("(a p) -> p a", p=P)),
                (A[:], A_log.rearrange("(a p) n -> p a n", p=P)),
                (s_gate, Wg.rearrange("(k p) e -> p k e", p=P)),
                (b_out[0:NE, :], be),
                (b_out[NE:NE + 1, :], fc2_b.rearrange("(a n) -> a n", a=1)),
            ]
            for k in range(KT):
                loads.append((s_exp[k].rearrange("p (e o) -> p e o", o=DM), We[:, k * P:(k + 1) * P, :].rearrange("e p o -> p e o")))
            for t in range(TB):
                loads.append((b_gate[:, t, :], bg.rearrange("(a n) -> a n", a=1).to_broadcast((P, NE))))
            assert len(loads) == N_LOADS

            def load(f):
                wait(sp, moe_first, f.count(16, -2 * 16 + TB))
                sp.dma_start(xin[:, f.part, :, :], x_v[f.index]).then_inc(x_loaded[f.part], 16)

            load(Chunk(0, 0))
            for dst, src in loads:
                sp.dma_start(dst, src, allow_slow_non_contiguous=True).then_inc(w_loaded, 16)

            def body(ck, has_back, has_front):
                if has_front:
                    load(ck.step(1))
                if has_back:
                    store(ck.step(-1))

            def store(b):
                wait(sp, out_ready, b.count(TB, TB))
                sp.dma_start(out_v[b.index], acc[:]).then_inc(out_stored, 16)

            over_chunks(sp, lambda f: None, body, lambda ck: store(ck.step(-1)))
            sp.wait_ge(out_stored, 16 * CHUNKS)

        @block.gpsimd
        def _(pool):
            pool.memset(ident[:], 0.0).then_inc(consts_set, 1)
            pool.memset(state[:], 0.0).then_inc(consts_set, 1)
            pool.memset(hist[:], 0.0).then_inc(consts_set, 1)
            pool.memset(half_neg[:], -0.5).then_inc(consts_set, 1)
            pool.memset(ones[:], 1.0).then_inc(consts_set, 1)
            pool.memset(gates[:, :, :, NE:NE + 1], 1.0).then_inc(consts_set, 1)
            for e in range(NE):
                pool.memset(prio[:, :, e:e + 1], float(NE - e)).then_inc(consts_set, 1)
            pool.wait_ge(consts_set, 1)
            pool.affine_select(out=ident[:], in_=ident[:], compare_op=ALU.not_equal, fill=1.0, base=0,
                               pattern=[[-1, P]], channel_multiplier=1).then_inc(consts_set, 1)
            pool.wait_ge(consts_set, 7 + NE)
            pool.wait_ge(w_loaded, 16 * N_LOADS)
            pool.wait_ge(A_exp, 1)
            pool.tensor_scalar(A[:], A[:], -1.0, 1.0, ALU.mult, ALU.mult).then_inc(consts_set, 1)

            def norm(f, part):
                if part == 0:
                    pool.wait_ge(ln_chain, f.count(N_LN, N_LN))
                    wait(pool, norm_chain, f.count(N_NORM))
                    apart(pool, passed)
                    pool.tensor_scalar(rstd[:, 0, :], mv[:, :, 1], EPS, 1.0, ALU.add, ALU.mult).then_inc(norm_chain, 1)
                    pool.tensor_scalar(rstd[:, 2, :], mv[:, :, 0], -1.0, 1.0, ALU.mult, ALU.mult).then_inc(norm_chain, 1)
                elif part == 1:
                    pool.wait_ge(norm_chain, f.count(N_NORM, 2))
                    pool.tensor_tensor(rstd[:, 1, :], rstd[:, 0, :], half_neg[:], ALU.pow).then_inc(norm_chain, 1)
                elif part == 2:
                    pool.wait_ge(norm_chain, f.count(N_NORM, 3))
                    pool.tensor_tensor(rstd[:, 0, :], rstd[:, 2, :], rstd[:, 1, :], ALU.mult).then_inc(norm_chain, 1)
                else:
                    pool.wait_ge(norm_chain, f.count(N_NORM, 4))
                    wait(pool, taps_ready, f.count(N_TAP))
                    wait(pool, conv_chain, f.count(N_CONV))
                    wait(pool, hist_saved, f.count(DT))
                    apart(pool, passed)
                    for t in range(TB) if part == 3 else ():
                        pool.tensor_scalar(xn[:, t, :], xin[:, f.part, t, :], rstd[:, 1, t:t + 1], rstd[:, 0, t:t + 1],
                                           ALU.mult, ALU.add).then_inc(norm_chain, 1)

            def clamp(f, k):
                pool.wait_ge(v_ready, f.count(DT, k + 1))
                pool.wait_ge(conv_chain, f.count(N_CONV, N_CONV))
                apart(pool, passed)
                pool.tensor_scalar(dt[:, f.part, k, :], wide[:, k, :], EXP_CAP, -BIG, ALU.min, ALU.max).then_inc(vmin_ready, 1)

            def times_u(f, k):
                pool.wait_ge(dt_ready, f.count(DT, k + 1))
                pool.tensor_tensor(wide[:, k, :], dt[:, f.part, k, :], u[:, f.part, k, :], ALU.mult).then_inc(du_ready, 1)

            def convolve(f, k, w):
                if w == 0:
                    pool.wait_ge(hist_set, f.count(DT, k + 1))
                    if k == 0:
                        wait(pool, yd_ready, f.count(DT * TB, -DT * TB))
                    pool.wait_ge(xc_ready, f.count(DT, k + 1))
                    apart(pool, passed)
                    pool.tensor_scalar(u[:, f.part, k, :], xc[:, k % 2, 0:CT], cw[:, k, 0:1], cb[:, k:k + 1],
                                       ALU.mult, ALU.add).then_inc(conv_chain, 1)
                else:
                    i = k * (TAPS - 1) + w - 1
                    pool.wait_ge(taps_ready, f.count(N_TAP, i + 1))
                    pool.wait_ge(conv_chain, f.count(N_CONV, k * TAPS + w))
                    pool.tensor_tensor(u[:, f.part, k, :], u[:, f.part, k, :], dt[:, f.part, i % DT, :], ALU.add).then_inc(conv_chain, 1)

            def gate_y(b, t):
                pool.wait_ge(yd_ready, b.count(DT * TB, DT * (t + 1)))
                pool.wait_ge(sz_ready, b.count(1, 1))
                cols = slice(t * P, (t + 1) * P)
                pool.tensor_tensor(wide[:, :, cols], wide[:, :, cols], sz[:, :, cols], ALU.mult).then_inc(yg_ready, 1)

            def scale_b(ck, n, t):
                if t == 0:
                    if n == 0:
                        pool.wait_ge(duT_ready, ck.count(TB, TB))
                        pool.wait_ge(bc_ready, ck.count(1, 1))
                    wait(pool, x_filled, ck.count(STEPS, DT * (n - 1)))
                    apart(pool, passed)
                pool.tensor_scalar(xb[:, n % 2, t, :], duT[:, ck.part, t, :], bc[:, ck.part, t, R + n:R + n + 1],
                                   1.0, ALU.mult, ALU.mult).then_inc(xb_ready, 1)

            def save_state(ck, n):
                wait(pool, scan_done, ck.count(STEPS, DT * (n + 1)))
                apart(pool, passed)
                pool.tensor_copy(state[:, slot_after(ck), n, :], h[:, n % 2, :, CT - 1]).then_inc(state_saved, 1)

            def steps(ck, has_back, has_front, has_steps=True):
                f, b = ck.step(1), ck.step(-1)
                for q in range(STEPS):
                    n = q // DT
                    if has_steps:
                        if n + 1 < NSTATE:
                            scale_b(ck, n + 1, q % DT)
                        if q % DT == 1:
                            if n > 0:
                                save_state(ck, n - 1)
                            elif not (ck.is_int() and ck.index == 0):
                                save_state(b, NSTATE - 1)
                    if has_back:
                        for t in range(TB):
                            if q == Q_YG[t] + 2:
                                gate_y(b, t)
                    if has_front:
                        if 0 <= q - Q_NORM < 4:
                            norm(f, q - Q_NORM)
                        for k in range(DT):
                            if 0 <= q - Q_CONV[k] < TAPS:
                                convolve(f, k, q - Q_CONV[k])
                            if q == Q_MIN[k]:
                                clamp(f, k)
                            if q == Q_DTU[k]:
                                times_u(f, k)
                        if q == Q_XB0:
                            for t in range(TB):
                                scale_b(f, 0, t)

            over_chunks(pool, lambda f: steps(f.step(-1), False, True, False), steps,
                        lambda ck: steps(ck, True, False, False))

        @block.scalar
        def _(act):
            act.wait_ge(w_loaded, 16 * N_LOADS)
            act.activation(A[:], A[:], ACT.Exp).then_inc(A_exp, 1)
            for i, (_, dst, src) in enumerate(prep_jobs):
                act.wait_ge(prep_filled, i + 1)
                act.copy(dst, src(ps_x[i % 2])).then_inc(prep_copied, 1)
            act.copy(w_gate[:, 0, :, :], s_gate).then_inc(split_done, 1)
            for k in range(KT):
                act.copy(w_exp[:, 0, k, :], s_exp[k]).then_inc(split_done, 1)
            act.wait_ge(split_done, N_SPLIT)

            def take(f, job):
                act.wait_ge(front_filled, f.count(NF, FRONT_AT[job] + 1))
                return ps_f[front_bank(f, job)]

            def front(f, q):
                for k in range(KT):
                    if q == Q_XNT[k] + 1:
                        if k == 0:
                            wait(act, side_filled, f.step(-2).count(NS, NS - NB))
                        bank = take(f, ("xnT", k))
                        act.copy(xnT[:, f.part, 0, k, :], bank[:]).then_inc(xnT_ready, 1)
                for k in range(DT):
                    if q == Q_XC[k] + 2:
                        bank = take(f, ("xc", k))
                        if k >= 2:
                            act.wait_ge(conv_chain, f.count(N_CONV, TAPS * (k - 2) + 1))
                            act.wait_ge(hist_saved, f.count(DT, k - 1))
                            act.wait_ge(taps_ready, f.count(N_TAP, (TAPS - 1) * (k - 1)))
                        act.activation(xc[:, k % 2, HIST:], bank[:], ACT.Identity, bias=b_xz[:, k:k + 1]).then_inc(xc_ready, 1)
                    if q == Q_CONV[k] - 1:
                        act.wait_ge(xc_ready, f.count(DT, k + 1))
                        act.wait_ge(hist_set, f.count(DT, k + 1))
                        if k == 0:
                            wait(act, dA_ready, f.count(STEPS, -STEPS))
                    if 0 < q - Q_CONV[k] + 2 < TAPS:
                        w = q - Q_CONV[k] + 2
                        i = k * (TAPS - 1) + w - 1
                        if i >= DT:
                            before = i - DT
                            act.wait_ge(conv_chain, f.count(N_CONV, before // (TAPS - 1) * TAPS + before % (TAPS - 1) + 2))
                        act.activation(dt[:, f.part, i % DT, :], xc[:, k % 2, w:w + CT], ACT.Identity,
                                       scale=cw[:, k, w:w + 1]).then_inc(taps_ready, 1)
                if q == Q_SILU:
                    act.wait_ge(conv_chain, f.count(N_CONV, N_CONV))
                    act.activation(u[:, f.part, :, :], u[:, f.part, :, :], ACT.Silu).then_inc(u_ready, 1)
                if q == Q_E2:
                    act.wait_ge(gate_chain, f.count(N_GATE, len(Q_TOP2)))
                    act.activation(gs[:, 4, :], gs[:, 3, :], ACT.Exp).then_inc(e2_ready, 1)
                if q == Q_XD[-1] + 1:
                    bank = take(f, ("xd", 0))
                    act.copy(xdT[:], bank[0:XD, :]).then_inc(xd_ready, 1)
                if q == Q_BC + 1:
                    bank = take(f, ("bc", 0))
                    wait(act, y_added, f.count(STEPS, -STEPS))
                    act.copy(bc[:, f.part, :, :], bank[:, 0:TB * XD].rearrange("p (t x) -> p t x", t=TB)).then_inc(bc_ready, 1)
                for k in range(DT):
                    if q == Q_DT[k] + 2:
                        bank = take(f, ("dt", k))
                        if k == 0:
                            wait(act, out_ready, f.count(TB, -TB))
                        act.activation(wide[:, k, :], bank[:], ACT.Identity, bias=b_dt[:, k:k + 1]).then_inc(v_ready, 1)
                if q == Q_SP:
                    act.wait_ge(vmin_ready, f.count(DT, DT))
                    act.activation(dt[:, f.part, :, :], dt[:, f.part, :, :], ACT.Exp).then_inc(sp_chain, 1)
                    act.wait_ge(sp_chain, f.count(2, 1))
                    act.activation(dt[:, f.part, :, :], dt[:, f.part, :, :], ACT.Ln, bias=1.0).then_inc(sp_chain, 1)
                for k in range(TB):
                    if q == Q_DUT[k] + 2:
                        bank = take(f, ("duT", k))
                        if k == 0:
                            wait(act, xb_ready, f.count(NSTATE * TB, -NSTATE * TB))
                        act.copy(duT[:, f.part, k, :], bank[:]).then_inc(duT_ready, 1)

            def decay(ck, q):
                n, k = q // DT, q % DT
                if q == 0:
                    act.wait_ge(dt_ready, ck.count(DT, DT))
                wait(act, scan_done, ck.count(STEPS, q - DT + 1))
                act.activation(dA[:, k, :], dt[:, ck.part, k, :], ACT.Exp, scale=A[:, k, n:n + 1]).then_inc(dA_ready, 1)

            def gate_z(ck, q):
                for k in range(DT):
                    if q == Q_Z[k] + 2:
                        job = ("z", k)
                        bank = side_bank(ck, job)
                        act.wait_ge(side_filled, side_count(ck, job, 1))
                        if k == 0:
                            wait(act, yg_ready, ck.count(TB))
                        act.activation(sz[:, k, :], ps_s[bank][:], ACT.Identity,
                                       bias=b_xz[:, DT + k:DT + k + 1]).then_inc(z_ready, 1)
                if q == Q_SILU:
                    act.wait_ge(z_ready, ck.count(DT, DT))
                    act.activation(sz[:], sz[:], ACT.Silu).then_inc(sz_ready, 1)
                    wait(act, probed, ck.count(1))
                    act.activation(ln_probe[:], ones[:], ACT.Ln).then_inc(probed, 1)

            def steps(ck, has_back, has_front, has_steps=True):
                f, b = ck.step(1), ck.step(-1)
                for q in range(STEPS):
                    if has_steps:
                        decay(ck, q)
                    if has_front:
                        front(f, q)
                    if has_steps:
                        gate_z(ck, q)
                    if has_back and q == Q_GT + 1:
                        act.wait_ge(side_filled, side_count(ck, ("gT", 0), 1))
                        act.copy(gT[:], ps_s[side_bank(ck, ("gT", 0))][0:NE + 1, :]).then_inc(gT_ready, 1)

            act.wait_ge(consts_set, N_CONSTS)
            over_chunks(act, lambda f: steps(f.step(-1), False, True, False), steps,
                        lambda ck: steps(ck, True, False, False))

        @block.vector
        def _(dve):
            def stats(f, q):
                for t in range(TB):
                    if q == Q_STATS[t]:
                        if t == 0:
                            dve.wait_ge(x_loaded[f.part], f.turn * 16 + 16)
                        dve.bn_stats(stat[:, t, :], xin[:, f.part, t, :]).then_inc(ln_chain, 1)
                if q == Q_AGGR:
                    dve.wait_ge(ln_chain, f.count(N_LN, TB))
                    wait(dve, norm_chain, f.count(N_NORM))
                    apart(dve, passed)
                    for t in range(TB):
                        dve.bn_aggr(mv[:, t, :], stat[:, t, :]).then_inc(ln_chain, 1)

            def top2(f, q):
                if q not in Q_TOP2 + Q_SHARE:
                    return
                n = (Q_TOP2 + Q_SHARE).index(q)

                def wide_of(col):
                    return gs[:, col, :].unsqueeze(2).to_broadcast([P, TB, NE])

                lg, eq, r, k1, l2, k2 = (gw[:, i, :, :] for i in range(6))
                if n == 0:
                    dve.wait_ge(front_filled, f.count(NF, FRONT_AT[("logit", 0)] + 1))
                    wait(dve, e2_ready, f.count(1))
                wait(dve, gate_chain, f.count(N_GATE, n))
                if n == len(Q_TOP2):
                    dve.wait_ge(e2_ready, f.count(1, 1))
                if n == N_GATE - 1:
                    wait(dve, gT_ready, f.count(1, -1))
                logits = ps_f[front_bank(f, ("logit", 0))][:, 0:TB * NE].rearrange("p (t e) -> p t e", t=TB)
                links = (
                    lambda: dve.tensor_tensor(lg, logits, b_gate[:], ALU.add),
                    lambda: dve.tensor_reduce(gs[:, 0, :], lg, AX_X, ALU.max),
                    lambda: dve.tensor_tensor(eq, lg, wide_of(0), ALU.is_equal),
                    lambda: dve.tensor_tensor(r, eq, prio[:], ALU.mult),
                    lambda: dve.tensor_reduce(gs[:, 1, :], r, AX_X, ALU.max),
                    lambda: dve.tensor_tensor(k1, r, wide_of(1), ALU.is_equal),
                    lambda: dve.scalar_tensor_tensor(l2, k1, -BIG, lg, ALU.mult, ALU.add),
                    lambda: dve.tensor_reduce(gs[:, 2, :], l2, AX_X, ALU.max),
                    lambda: dve.tensor_tensor(eq, l2, wide_of(2), ALU.is_equal),
                    lambda: dve.tensor_tensor(r, eq, prio[:], ALU.mult),
                    lambda: dve.tensor_reduce(gs[:, 1, :], r, AX_X, ALU.max),
                    lambda: dve.tensor_tensor(k2, r, wide_of(1), ALU.is_equal),
                    lambda: dve.tensor_tensor(gs[:, 3, :], gs[:, 2, :], gs[:, 0, :], ALU.subtract),
                    lambda: dve.tensor_scalar(gs[:, 5, :], gs[:, 4, :], 1.0, None, ALU.add),
                    lambda: dve.reciprocal(gs[:, 6, :], gs[:, 5, :]),
                    lambda: dve.tensor_tensor(gs[:, 7, :], gs[:, 4, :], gs[:, 6, :], ALU.mult),
                    lambda: dve.tensor_tensor(eq, k1, wide_of(6), ALU.mult),
                    lambda: dve.tensor_tensor(r, k2, wide_of(7), ALU.mult),
                    lambda: dve.tensor_tensor(gates[:, f.part, :, 0:NE], eq, r, ALU.add),
                )
                assert len(links) == N_GATE
                links[n]().then_inc(gate_chain, 1)

            def front(f, q):
                stats(f, q)
                top2(f, q)
                for k in range(KT):
                    if q == Q_XNT[k] + 1:
                        bank = front_bank(f, ("xnT", k))
                        dve.wait_ge(front_filled, f.count(NF, FRONT_AT[("xnT", k)] + 1))
                        dve.wait_ge(xnT_ready, f.count(KT, k + 1))
                        dve.tensor_tensor(xnT[:, f.part, 1, k, :], ps_f[bank][:], xnT[:, f.part, 0, k, :].bitcast(F32),
                                          ALU.subtract).then_inc(xnL_ready, 1)
                for k in range(DT):
                    if q == Q_XC[k]:
                        if k < 2:
                            dve.wait_ge(front_filled, f.count(NF, FRONT_AT[("xnT", KT - 1)] + 1))
                        else:
                            dve.wait_ge(conv_chain, f.count(N_CONV, TAPS * (k - 2) + 1))
                            dve.wait_ge(taps_ready, f.count(N_TAP, (TAPS - 1) * (k - 1)))
                        wait(dve, hist_saved, f.count(DT, max(k - 1, 0)))
                        dve.tensor_copy(xc[:, k % 2, 0:HIST], hist[:, slot_before(f), k, :]).then_inc(hist_set, 1)
                    if q == Q_XC[k] + 3:
                        dve.wait_ge(xc_ready, f.count(DT, k + 1))
                        dve.tensor_copy(hist[:, slot_after(f), k, :], xc[:, k % 2, CT:CT + HIST]).then_inc(hist_saved, 1)
                for k in range(DT):
                    if q == Q_MAX[k]:
                        if k == 0:
                            dve.wait_ge(sp_chain, f.count(2, 2))
                        dve.tensor_tensor(dt[:, f.part, k, :], dt[:, f.part, k, :], wide[:, k, :], ALU.max).then_inc(dt_ready, 1)

            def back(ck, q):
                b = ck.step(-1)
                for t in range(TB):
                    if q == Q_YG[t] + 1:
                        job = ("yg", t)
                        bank = side_bank(ck, job)
                        dve.wait_ge(side_filled, side_count(ck, job, 1))
                        for k in range(DT):
                            cols = slice(t * P, (t + 1) * P)
                            dve.scalar_tensor_tensor(wide[:, k, cols], u[:, b.part, k, cols], d_col[:, k:k + 1],
                                                     ps_s[bank][:, k * P:(k + 1) * P], ALU.mult, ALU.add).then_inc(yd_ready, 1)
                for t in range(TB):
                    if q == Q_OUT[t][-1] + 1:
                        job = ("out", t)
                        dve.wait_ge(side_filled, side_count(ck, job, 1))
                        dve.wait_ge(moe_second, b.count(16, 16))
                        dve.tensor_tensor(acc[:, t, :], ps_s[side_bank(ck, job)][:, 0:DM], acc[:, t, :], ALU.add).then_inc(out_ready, 1)

            def experts(ck, q):
                for i in range(16):
                    pair, t = i // TB, i % TB
                    if q not in (Q_MOE[i] + 1, Q_MOE[i] + 2):
                        continue
                    j = q - Q_MOE[i] - 1
                    e = 2 * pair + j
                    if j == 0:
                        if i == 0:
                            wait(dve, out_stored, ck.count(16))
                            dve.wait_ge(gate_chain, ck.count(N_GATE, N_GATE))
                        dve.wait_ge(side_filled, side_count(ck, ("moe", i), 1))
                        if pair > 0:
                            dve.wait_ge(moe_second, ck.count(16, i - TB + 1))
                    else:
                        dve.wait_ge(moe_first, ck.count(16, i + 1))
                    dve.scalar_tensor_tensor(acc[:, t, :], ps_s[side_bank(ck, ("moe", i))][:, j * DM:(j + 1) * DM],
                                             gates[:, ck.part, t, e:e + 1],
                                             xin[:, ck.part, t, :] if e == 0 else acc[:, t, :],
                                             ALU.mult, ALU.add).then_inc(moe_second if j else moe_first, 1)

            def scan(ck, q):
                n, k = q // DT, q % DT
                if k == 0:
                    wait(dve, h_filled, ck.count(STEPS, DT * (n - 1)))
                    wait(dve, state_saved, ck.count(NSTATE, n - 1))
                dve.wait_ge(dA_ready, ck.count(STEPS, q + 1))
                dve.wait_ge(x_filled, ck.count(STEPS, q + 1))
                dve.tensor_tensor_scan(h[:, n % 2, k, :], dA[:, k, :], ps_x[q % 2][:],
                                       state[:, slot_before(ck), n, k:k + 1], ALU.mult, ALU.add).then_inc(scan_done, 1)

            def add_y(ck, n, t):
                i = DT * n + t
                dve.wait_ge(h_filled, ck.count(STEPS, i + 1))
                if n == 0:
                    if t == 0:
                        dve.wait_ge(bc_ready, ck.count(1, 1))
                    wait(dve, side_filled, side_count(ck, ("yg", t), 1))
                    dve.tensor_scalar(yT[:, t, :], ps_h[t % 2][:], bc[:, ck.part, t, R + NSTATE:R + NSTATE + 1],
                                      None, ALU.mult).then_inc(y_added, 1)
                else:
                    dve.wait_ge(y_added, ck.count(STEPS, i - TB + 1))
                    dve.scalar_tensor_tensor(yT[:, t, :], ps_h[t % 2][:],
                                             bc[:, ck.part, t, R + NSTATE + n:R + NSTATE + n + 1],
                                             yT[:, t, :], ALU.mult, ALU.add).then_inc(y_added, 1)

            def steps(ck, has_back, has_front, has_steps=True):
                f, b = ck.step(1), ck.step(-1)
                for q in range(STEPS):
                    if has_steps:
                        scan(ck, q)
                    if q >= DT:
                        if has_steps:
                            add_y(ck, q // DT - 1, q % DT)
                    elif has_back or (has_steps and not (ck.is_int() and ck.index == 0)):
                        add_y(b, NSTATE - 1, q)
                    if has_front:
                        front(f, q)
                    if has_back:
                        back(ck, q)
                    if has_steps:
                        experts(ck, q)

            dve.wait_ge(w_loaded, 16 * N_LOADS)
            for i, half in ((i, half) for i in range(KT) for half in range(2)):
                job = JOIN_AT + 2 * i + half
                dve.wait_ge(prep_copied, job + 1)
                cols = slice(half * 512, (half + 1) * 512)
                dve.tensor_tensor(w_xz[:, 1, i, cols], ps_x[job % 2][:], w_xz[:, 0, i, cols].bitcast(F32),
                                  ALU.subtract).then_inc(prep_split, 1)
            dve.wait_ge(split_done, 1 + KT)
            dve.tensor_tensor(w_gate[:, 1, :, :], s_gate, w_gate[:, 0, :, :].bitcast(F32), ALU.subtract).then_inc(split_done, 1)
            for k in range(KT):
                dve.tensor_tensor(w_exp[:, 1, k, :], s_exp[k], w_exp[:, 0, k, :].bitcast(F32),
                                  ALU.subtract).then_inc(split_done, 1)
            dve.wait_ge(split_done, N_SPLIT)
            dve.wait_ge(consts_set, N_CONSTS)
            over_chunks(dve, lambda f: steps(f.step(-1), False, True, False), steps,
                        lambda ck: steps(ck, True, False, False))

        @block.tensor
        def _(pe):
            pe.wait_ge(w_loaded, 16 * N_LOADS)
            pe.wait_ge(consts_set, N_CONSTS)
            for i, (fill, _, _) in enumerate(prep_jobs):
                wait(pe, prep_copied, i - 1)
                wait(pe, prep_split, min(max(i - 1 - JOIN_AT, 0), 2 * KT))
                last = fill(pe, ps_x[i % 2])
                last.then_inc(prep_filled, 1)
            pe.wait_ge(prep_copied, len(prep_jobs))
            pe.wait_ge(split_done, N_SPLIT)

            def mm(out, lhsT, rhs, k, n):
                return pe.matmul(out, lhsT, rhs, start=k == 0, stop=k == n - 1)

            def mm_halves(out, lhsT, rhs):
                passes = [(a, b, i) for i in range(KT) for a, b in ((0, 0), (0, 1), (1, 0))]
                for n, (a, b, i) in enumerate(passes):
                    last = mm(out, lhsT(a, i), rhs(b, i), n, len(passes))
                return last

            def xn_rows(part, t):
                return lambda half, i: xnT[:, part, half, i, t * P:(t + 1) * P]

            def inner(of, bank, e):
                return mm_halves(bank[:], lambda half, i: w_xz[:, half, i, e * P:(e + 1) * P],
                                 lambda half, i: xnT[:, of.part, half, i, :])

            def fill_front(f, job, part):
                kind, k = job
                bank = ps_f[front_bank(f, job)]
                if part == 0:
                    before = two_before(f, job, FRONT, FRONT_AT)
                    if not (before[0].is_int() and before[0].index < 0):
                        wait(pe, *front_taken(*before))
                if kind == "xnT":
                    pe.wait_ge(norm_chain, f.count(N_NORM, N_NORM))
                    for t in range(TB):
                        last = pe.transpose(bank[:, t * P:(t + 1) * P], xn[:, t, k * P:(k + 1) * P], ident[:])
                elif kind == "logit":
                    for t in range(TB):
                        last = mm_halves(bank[:, t * NE:(t + 1) * NE], xn_rows(f.part, t), lambda half, i: w_gate[:, half, i, :])
                elif kind == "xc":
                    if k == 0:
                        pe.wait_ge(xnT_ready, f.count(KT, KT))
                        pe.wait_ge(xnL_ready, f.count(KT, KT))
                    last = inner(f, bank, k)
                elif kind == "xd":
                    if part == 0:
                        pe.wait_ge(u_ready, f.count(1, 1))
                    last = mm(bank[0:XD, :], w_xd[:, part, :], u[:, f.part, part, :], part, DT)
                    if part < DT - 1:
                        return
                elif kind == "bc":
                    pe.wait_ge(xd_ready, f.count(1, 1))
                    apart(pe, passed)
                    for t in range(TB):
                        last = pe.transpose(bank[:, t * XD:(t + 1) * XD], xdT[:, t * P:(t + 1) * P], ident[0:XD, 0:XD])
                elif kind == "dt":
                    last = mm(bank[:], w_dt[:, k * P:(k + 1) * P], xdT[0:R, :], 0, 1)
                else:
                    pe.wait_ge(du_ready, f.count(DT, DT))
                    for i in range(DT):
                        last = pe.transpose(bank[:, i * P:(i + 1) * P], wide[:, i, k * P:(k + 1) * P], ident[:])
                last.then_inc(front_filled, 1)

            def fill_side(ck, job, part):
                kind, k = job
                b = ck.step(-1)
                bank = ps_s[side_bank(ck, job)]
                if part == 0:
                    before = two_before(ck, job, SIDE, SIDE_AT)
                    if not (before[0].is_int() and (before[0].index < 0 or before[0].index == 0 and before[1] in BACK)):
                        wait(pe, *side_taken(*before))
                if kind == "gT":
                    pe.wait_ge(gate_chain, b.count(N_GATE, N_GATE))
                    for t in range(TB):
                        last = pe.transpose(bank[0:NE + 1, t * P:(t + 1) * P], gates[:, b.part, t, :], ident[:])
                elif kind == "yg":
                    pe.wait_ge(y_added, b.count(STEPS, STEPS - TB + k + 1))
                    for i in range(DT):
                        last = pe.transpose(bank[:, i * P:(i + 1) * P], yT[:, k, i * P:(i + 1) * P], ident[:])
                elif kind == "out":
                    if part == 0:
                        pe.wait_ge(yg_ready, b.count(TB, k + 1))
                        pe.wait_ge(gT_ready, b.count(1, 1))
                    for i in ((0, 1), (2, 3))[part]:
                        mm(bank[:, 0:DM], wide[:, i, k * P:(k + 1) * P], w_out[:, i, :], i, DT + 1)
                    if part == 0:
                        return
                    last = mm(bank[:, 0:DM], gT[:, k * P:(k + 1) * P], b_out[:], DT, DT + 1)
                elif kind == "z":
                    last = inner(ck, bank, DT + k)
                else:
                    pair, t = k // TB, k % TB
                    last = mm_halves(bank[:], xn_rows(ck.part, t), lambda half, i: w_exp[:, half, i, pair * 2 * DM:(pair + 1) * 2 * DM])
                last.then_inc(side_filled, 1)

            def places(jobs, at):
                return {job: where if isinstance(where, tuple) else (where,) for job, where in zip(jobs, at)}

            places_f = places(FRONT, (*Q_XNT, *Q_XC[0:2], Q_LOGIT, *Q_XC[2:4], Q_XD, Q_BC, *Q_DT, *Q_DUT))
            places_s = places(SIDE, (Q_GT, *Q_YG, *Q_OUT, *sorted(Q_Z + Q_MOE)))

            def turn_x(ck, q):
                n, k = q // DT, q % DT
                if k == 0:
                    pe.wait_ge(xb_ready, ck.count(NSTATE * TB, TB * (n + 1)))
                wait(pe, scan_done, ck.count(STEPS, q - 1))
                for t in range(TB):
                    last = pe.transpose(ps_x[q % 2][:, t * P:(t + 1) * P], xb[:, n % 2, t, k * P:(k + 1) * P], ident[:])
                last.then_inc(x_filled, 1)

            def turn_h(ck, n, t):
                i = DT * n + t
                if t == 0:
                    pe.wait_ge(scan_done, ck.count(STEPS, DT * (n + 1)))
                wait(pe, y_added, ck.count(STEPS, i - 1))
                for k in range(DT):
                    last = pe.transpose(ps_h[t % 2][:, k * P:(k + 1) * P], h[:, n % 2, k, t * P:(t + 1) * P], ident[:])
                last.then_inc(h_filled, 1)

            def steps(ck, has_back, has_front, has_steps=True):
                f, b = ck.step(1), ck.step(-1)
                for q in range(STEPS):
                    if has_steps:
                        turn_x(ck, q)
                    if q >= DT:
                        if has_steps:
                            turn_h(ck, q // DT - 1, q % DT)
                    elif has_back or (has_steps and not (ck.is_int() and ck.index == 0)):
                        turn_h(b, NSTATE - 1, q)
                    if has_front:
                        for job in FRONT:
                            if q in places_f[job]:
                                fill_front(f, job, places_f[job].index(q))
                    for job in SIDE:
                        if q in places_s[job] and (has_back if job in BACK else has_steps):
                            fill_side(ck, job, places_s[job].index(q))

            over_chunks(pe, lambda f: steps(f.step(-1), False, True, False), steps,
                        lambda ck: steps(ck, True, False, False))


_INS = ['x', 'fc1_w', 'fc1_b', 'in_proj_w', 'conv_w', 'conv_b', 'x_proj_w', 'dt_proj_w', 'dt_proj_b',
        'A_log', 'D', 'out_proj_w', 'fc2_w', 'fc2_b']
_INS = ['L0_attn_' + n for n in _INS] + ['L0_ffn_We', 'L0_ffn_be', 'L0_ffn_Wg', 'L0_ffn_bg']


def kernel(**inputs):
    import numpy as _np
    import concourse.bacc as _bacc
    from concourse import mybir as _mybir
    from concourse.bass_utils import run_bass_kernel_spmd as _run

    nc = _bacc.Bacc("TRN2", target_bir_lowering=False, num_devices=1)
    arrays, args = {}, []
    for name in _INS:
        a = _np.ascontiguousarray(inputs[name])
        arrays[f"in_{name}_dram"] = a
        args.append(nc.dram_tensor(f"in_{name}_dram", a.shape, _mybir.dt.from_np(a.dtype), kind="ExternalInput").ap())
    shape = inputs['L0_attn_x'].shape
    args.append(nc.dram_tensor("out_0_dram", shape, _mybir.dt.float32, kind="ExternalOutput").ap())
    mamba_moe_kernel(nc, *args)
    r = _run(nc, [arrays], core_ids=[0])
    return r.results[0]["out_0_dram"]
```

```python
import concourse.bass as bass
from concourse import mybir
from contextlib import ExitStack

P = 128
F32 = mybir.dt.float32
F32R = mybir.dt.float32r
ALU = mybir.AluOpType
ACT = mybir.ActivationFunctionType
AX_X = mybir.AxisListType.X

EPS = 1e-5
BIG = 3.0e38
EXP_CAP = 40.0
EXP_AND_LN = 6
RATIO = 2

Q_XNT = ((0,), (1,))
Q_GT = (1,)
Q_YG = ((2,), (3,), (4,), (5,))
Q_XC = ((6, 7), (8, 9), (14, 15), (20, 21))
Q_LOGIT = (11,)
Q_Z = ((10, 12), (16, 17), (22, 23), (25, 26))
Q_OUT = ((12, 13, 14), (18, 19, 20), (23, 24, 25), (27, 28, 29))
Q_XD = (34, 35, 36, 37)
Q_BC = (40,)
Q_DT = ((41,), (42,), (43,), (44,))
Q_DUT = ((53,), (54,), (55,), (56,))
Q_MOE = tuple((q,) for q in range(30, 64) if q not in (34, 36))
Q_CONV = (10, 14, 18, 24)
Q_TOP2 = tuple(range(13, 26))
Q_E2 = 27
Q_SHARE = (29, 30, 31, 32, 33, 34)
Q_SILU = 30
Q_MIN = (44, 45, 46, 47)
Q_SP = (45, 46, 47, 48)
Q_MAX = (47, 48, 49, 50)
Q_DTU = (48, 49, 50, 51)
Q_UD = (35, 37, 39, 41)
Q_STATS = (48, 49, 50, 51)
Q_AGGR = 52
Q_NORM = 53
Q_XB0 = 60

XNT, LOGIT, XC, XDBL, BC, DELTA, DUT = "xnT", "logit", "xc", "xd", "bc", "dt", "duT"
GT, YG, OUT, Z, MOE = "gT", "yg", "out", "z", "moe"


def in_order(places):
    jobs = sorted(places, key=lambda job: (places[job][-1], job))
    assert all(places[job][-1] <= places[later][0] for job, later in zip(jobs, jobs[2:]))
    return jobs


def numbered(kind, places):
    return {(kind, k): at for k, at in enumerate(places)}


FRONT_PLACES = {**numbered(XNT, Q_XNT), **numbered(XC, Q_XC), (LOGIT, 0): Q_LOGIT, (XDBL, 0): Q_XD, (BC, 0): Q_BC,
                **numbered(DELTA, Q_DT), **numbered(DUT, Q_DUT)}
BACK_PLACES = {(GT, 0): Q_GT, **numbered(YG, Q_YG), **numbered(OUT, Q_OUT)}
SIDE_PLACES = {**BACK_PLACES, **numbered(Z, Q_Z), **numbered(MOE, Q_MOE)}
FRONT, SIDE = in_order(FRONT_PLACES), in_order(SIDE_PLACES)
NF, NB, NS = len(FRONT), len(BACK_PLACES), len(SIDE)
FRONT_AT = {job: i for i, job in enumerate(FRONT)}
SIDE_AT = {job: i for i, job in enumerate(SIDE)}


class Chunk:

    def __init__(self, turn, part):
        self.turn, self.part = turn, part
        self.index = turn * RATIO + part

    def count(self, per, more=0):
        return self.turn * (RATIO * per) + (self.part * per + more)

    def step(self, by):
        part = self.part + by
        return Chunk(self.turn + part // RATIO, part % RATIO)

    def is_int(self):
        return isinstance(self.turn, int)


def wait(eng, sem, value):
    if isinstance(value, int) and value <= 0:
        return
    eng.wait_ge(sem, value)


def apart(eng, passed):
    eng.nop().then_inc(passed, 1)


def mamba_moe_kernel(nc, x, fc1_w, fc1_b, in_proj_w, conv_w, conv_b, x_proj_w, dt_proj_w, dt_proj_b,
                     A_log, D, out_proj_w, fc2_w, fc2_b, We, be, Wg, bg, out):
    B, L, DM = x.shape
    DI, NSTATE = A_log.shape
    TAPS = conv_w.shape[1]
    R = dt_proj_w.shape[1]
    XD = R + 2 * NSTATE
    NE = Wg.shape[1]
    KT, DT, ET = DM // P, DI // P, 2 * DI // P
    CT = 512
    TB = CT // P
    CHUNKS = B * L // CT
    PER_BATCH = L // CT
    STEPS = NSTATE * DT
    HIST = TAPS - 1
    G0 = 64
    assert DM == 256 and DI == 512 and TB == DT == 4 and PER_BATCH == 2 * RATIO and CHUNKS % RATIO == 0
    TURNS = CHUNKS // RATIO

    x_v = x.rearrange("b (c t p) d -> (b c) p t d", t=TB, p=P)
    out_v = out.rearrange("b (c t p) d -> (b c) p t d", t=TB, p=P)

    with ExitStack() as ctx:
        def sb(name, shape, dtype=F32):
            return ctx.enter_context(nc.sbuf_tensor(name, shape, dtype))

        def sem(name):
            return ctx.enter_context(nc.semaphore(name))

        ident = sb("ident", [P, P])
        w_xz = sb("w_xz", [P, 2, KT, 2 * DI], F32R)
        b_xz = sb("b_xz", [P, ET])
        w_xd = sb("w_xd", [P, DT, XD])
        w_dt = sb("w_dt", [R, DI])
        w_out = sb("w_out", [P, DT, DM])
        w_exp = sb("w_exp", [P, 2, KT, NE * DM], F32R)
        b_out = sb("b_out", [P, DM])[G0:G0 + NE + 1, :]
        w_gate = sb("w_gate", [P, 2, KT, NE], F32R)
        b_gate = sb("b_gate", [P, TB, NE])
        prio = sb("prio", [P, TB, NE])
        cw = sb("cw", [P, DT, TAPS])
        cb = sb("cb", [P, DT])
        b_dt = sb("b_dt", [P, DT])
        d_col = sb("d_col", [P, DT])
        f1b = sb("f1b", [P, KT])
        A = sb("A", [P, DT, NSTATE])
        half_neg = sb("half_neg", [P, TB])

        xin = sb("xin", [P, 2, TB, DM])
        xc = sb("xc", [P, 2, HIST + CT])
        xn = xc[:].rearrange("p a b -> p (a b)")[:, 0:TB * DM].rearrange("p (t d) -> p t d", t=TB)
        xnT = sb("xnT", [P, 2, 2, KT, CT], F32R)
        u = sb("u", [P, 2, DT, CT])
        sz = sb("sz", [P, DT, CT])
        dt = sb("dt", [P, 2, DT, CT])
        wide = sb("wide", [P, DT, CT])
        duT = sb("duT", [P, 2, TB, DI])
        bc = sb("bc", [P, 2, TB, XD])
        small = sb("small", [P, CT])
        xdT = small[0:XD, :]
        gates = sb("gates", [P, 2, TB, NE + 1])
        gT = small[G0:G0 + NE + 1, :]
        acc = sb("acc", [P, TB, DM])
        stat = sb("stat", [P, TB, 6])
        mv = sb("mv", [P, TB, 2])
        rstd = sb("rstd", [P, 3, TB])
        gw = sb("gw", [P, 8, TB, NE])
        gs = sb("gs", [P, 8, TB])
        hist = sb("hist", [P, 3, DT, HIST])
        state = sb("state", [P, 3, NSTATE, DT])
        xb = sb("xb", [P, 2, TB, DI])
        dA = sb("dA", [P, DT, CT])
        h = sb("h", [P, 2, DT, CT])
        yT = sb("yT", [P, TB, DI])

        s_inp = xb[:, 0, :, :].rearrange("p a b -> p (a b)")[:, 0:ET * DM].rearrange("p (e m) -> p e m", m=DM)
        s_fc1 = xb[:, 1, 0, :].rearrange("p (m i) -> p m i", m=KT)
        s_fc2 = xb[:, 1, 1, :].rearrange("p (o m) -> p o m", o=KT)
        s_outp = xb[:, 1, 2:4, :]
        s_xp = dA[0:XD, 0, :]
        s_dt = dA[:, 1, 0:DT * R].rearrange("p (a r) -> p a r", a=DT)
        s_inT = h[:, 0, :, :].rearrange("p a b -> p (a b)").rearrange("p (m e) -> p m e", m=KT)
        s_exp = [yT[:].rearrange("p a b -> p (a b)"), u[:, 0, :, :].rearrange("p a b -> p (a b)")]
        s_gate = dA[:, 2, 0:KT * NE].rearrange("p (k e) -> p k e", e=NE)
        s_fc2T = h[:, 1, 0, :].rearrange("p (m o) -> p m o", m=KT)

        def psum(name):
            return ctx.enter_context(nc.psum_tensor(name, [P, 512], F32))

        ps_x = [psum(f"ps_x{i}") for i in range(2)]
        ps_h = [psum(f"ps_h{i}") for i in range(2)]
        ps_f = [psum(f"ps_f{i}") for i in range(2)]
        ps_s = [psum(f"ps_s{i}") for i in range(2)]

        passed = sem("passed")
        w_loaded = sem("w_loaded")
        consts_set = sem("consts_set")
        A_exp = sem("A_exp")
        prep_filled = sem("prep_filled")
        prep_copied = sem("prep_copied")
        prep_split = sem("prep_split")
        x_loaded = [sem(f"x_loaded{i}") for i in range(RATIO)]
        out_stored = [sem(f"out_stored{t}") for t in range(4)]
        ln_chain = sem("ln_chain")
        norm_chain = sem("norm_chain")
        gate_chain = sem("gate_chain")
        e2_ready = sem("e2_ready")
        front_filled = sem("front_filled")
        side_filled = sem("side_filled")
        xnT_ready = sem("xnT_ready")
        hist_set = sem("hist_set")
        hist_saved = sem("hist_saved")
        xc_ready = sem("xc_ready")
        z_ready = sem("z_ready")
        taps_ready = sem("taps_ready")
        conv_chain = sem("conv_chain")
        xnL_ready = sem("xnL_ready")
        split_done = sem("split_done")
        u_ready = sem("u_ready")
        sz_ready = sem("sz_ready")
        xd_ready = sem("xd_ready")
        bc_ready = sem("bc_ready")
        v_ready = sem("v_ready")
        vmin_ready = sem("vmin_ready")
        e_ready = sem("e_ready")
        ln_ready = sem("ln_ready")
        dt_ready = sem("dt_ready")
        du_ready = sem("du_ready")
        duT_ready = sem("duT_ready")
        xb_ready = sem("xb_ready")
        x_filled = sem("x_filled")
        dA_ready = sem("dA_ready")
        scan_done = sem("scan_done")
        state_saved = sem("state_saved")
        h_filled = sem("h_filled")
        y_added = sem("y_added")
        gT_ready = sem("gT_ready")
        ud_ready = sem("ud_ready")
        yd_ready = sem("yd_ready")
        yg_ready = sem("yg_ready")
        moe_added = sem("moe_added")
        out_ready = sem("out_ready")

        N_LOADS = 15 + KT + TB
        N_CONSTS = 5 + NE + 1 + 1

        def turn_in(m, half):
            def fill(pe, bank):
                for i in range(4):
                    last = pe.transpose(bank[:, i * P:(i + 1) * P], s_inp[:, 4 * half + i, m * P:(m + 1) * P], ident[:])
                return last
            return fill, s_inT[:, m, half * 512:(half + 1) * 512], lambda bank: bank[:]

        def turn_fc2(m):
            def fill(pe, bank):
                for o in range(KT):
                    last = pe.transpose(bank[:, o * P:(o + 1) * P], s_fc2[:, o, m * P:(m + 1) * P], ident[:])
                return last
            return fill, s_fc2T[:, m, :], lambda bank: bank[:, 0:DM]

        def turn_xd(pe, bank):
            for i in range(DT):
                last = pe.transpose(bank[:, i * XD:(i + 1) * XD], s_xp[:, i * P:(i + 1) * P], ident[0:XD, 0:XD])
            return last

        def turn_dt(pe, bank):
            for i in range(DT):
                last = pe.transpose(bank[0:R, i * P:(i + 1) * P], s_dt[:, i, :], ident[:])
            return last

        def join_in(i, half):
            def fill(pe, bank):
                pe.wait_ge(prep_copied, 4)
                for m in range(KT):
                    last = pe.matmul(bank[:], s_fc1[:, m, i * P:(i + 1) * P], s_inT[:, m, half * 512:(half + 1) * 512],
                                     start=m == 0, stop=m == KT - 1)
                return last
            return fill, w_xz[:, 0, i, half * 512:(half + 1) * 512], lambda bank: bank[:]

        def join_bias(pe, bank):
            for e in range(ET):
                for m in range(KT):
                    last = pe.matmul(bank[:, e:e + 1], s_inT[:, m, e * P:(e + 1) * P], f1b[:, m:m + 1],
                                     start=m == 0, stop=m == KT - 1)
            return last

        def join_out(a):
            def fill(pe, bank):
                pe.wait_ge(prep_copied, 6)
                for m in range(KT):
                    last = pe.matmul(bank[:, 0:DM], s_outp[:, m, a * P:(a + 1) * P], s_fc2T[:, m, :],
                                     start=m == 0, stop=m == KT - 1)
                return last
            return fill, w_out[:, a, :], lambda bank: bank[:, 0:DM]

        N_SPLIT = 1 + KT + 1 + KT
        JOIN_AT = 2 * KT + KT + 2

        prep_jobs = ([turn_in(m, half) for m in range(KT) for half in range(2)] + [turn_fc2(m) for m in range(KT)]
                     + [(turn_xd, w_xd[:], lambda bank: bank[:, 0:DT * XD].rearrange("p (a x) -> p a x", a=DT)),
                        (turn_dt, w_dt[:], lambda bank: bank[0:R, :])]
                     + [join_in(i, half) for i in range(KT) for half in range(2)]
                     + [(join_bias, b_xz[:], lambda bank: bank[:, 0:ET])] + [join_out(a) for a in range(DT)])

        block = ctx.enter_context(nc.Block())

        N_LN = 2 * TB
        N_MOE = NE * TB
        N_TAP = DT * (TAPS - 1)
        N_CONV = DT * TAPS
        N_NORM = 4 + TB
        N_GATE = len(Q_TOP2) + len(Q_SHARE)

        def side_count(ck, job):
            filled = SIDE[:SIDE_AT[job] + 1]
            if ck.is_int() and ck.index == 0:
                return len([other for other in filled if side_ran(ck, other)])
            return ck.count(NS, len([other for other in filled if side_ran(ck, other)]) - NB)

        def side_bank(ck, job):
            return (ck.part * NS + SIDE_AT[job]) % 2

        def front_bank(f, job):
            return (f.part * NF + FRONT_AT[job]) % 2

        def front_taken(f, job):
            kind, k = job
            return {
                XNT: (xnL_ready, f.count(KT, k + 1)), XC: (xc_ready, f.count(DT, k + 1)),
                LOGIT: (gate_chain, f.count(N_GATE, 1)), XDBL: (xd_ready, f.count(1, 1)),
                BC: (bc_ready, f.count(1, 1)), DELTA: (v_ready, f.count(DT, k + 1)),
                DUT: (duT_ready, f.count(TB, k + 1)),
            }[kind]

        def side_taken(ck, job):
            kind, k = job
            b = ck.step(-1)
            return {
                GT: (gT_ready, b.count(1, 1)), YG: (yd_ready, b.count(TB, k + 1)),
                OUT: (out_ready, b.count(TB, k + 1)), Z: (z_ready, ck.count(DT, k + 1)),
                MOE: (moe_added, ck.count(N_MOE, k + 1)),
            }[kind]

        def two_before(ck, job, order, at, ran):
            i = at[job] - 2
            while i >= -2 * len(order):
                c, other = (ck, order[i]) if i >= 0 else (ck.step(i // len(order)), order[i % len(order)])
                if ran(c, other):
                    return c, other
                i -= 2
            return None

        def front_ran(c, job):
            return not c.is_int() or c.index >= 0

        def side_ran(c, job):
            if not c.is_int():
                return True
            return 0 < c.index <= CHUNKS if job in BACK_PLACES else 0 <= c.index < CHUNKS

        def slot_before(ck):
            if ck.part == 1:
                return 2
            return ck.turn % 2

        def slot_after(ck):
            return 2 if ck.part == 0 else 1

        def over_chunks(eng, front0, body, last):
            front0()
            for part in range(RATIO):
                body(Chunk(0, part), has_back=part > 0)
            with eng.Fori(1, TURNS - 1) as turn:
                for part in range(RATIO):
                    body(Chunk(turn, part))
            for part in range(RATIO):
                body(Chunk(TURNS - 1, part), has_front=part < RATIO - 1, has_norm=False)
            last(Chunk(TURNS, 0))

        def around(steps):
            def before_first():
                steps(Chunk(-1, 0), has_back=False, has_front=False, has_steps=False)
                steps(Chunk(-1, 1), has_back=False, has_steps=False)

            def behind_last(ck):
                steps(ck, has_front=False, has_norm=False, has_steps=False)
            return before_first, behind_last

        @block.sync
        def _(sp):
            loads = [
                (s_inp, in_proj_w.rearrange("(e p) m -> p e m", p=P)),
                (s_fc1, fc1_w.rearrange("(m p) i -> p m i", p=P)),
                (s_fc2, fc2_w.rearrange("(o p) m -> p o m", p=P)),
                (s_outp, out_proj_w.rearrange("(m p) d -> p m d", p=P)),
                (s_xp, x_proj_w),
                (s_dt, dt_proj_w.rearrange("(a p) r -> p a r", p=P)),
                (f1b[:], fc1_b.rearrange("(m p) -> p m", p=P)),
                (cw[:], conv_w.rearrange("(a p) w -> p a w", p=P)),
                (cb[:], conv_b.rearrange("(a p) -> p a", p=P)),
                (b_dt[:], dt_proj_b.rearrange("(a p) -> p a", p=P)),
                (d_col[:], D.rearrange("(a p) -> p a", p=P)),
                (A[:], A_log.rearrange("(a p) n -> p a n", p=P)),
                (s_gate, Wg.rearrange("(k p) e -> p k e", p=P)),
                (b_out[0:NE, :], be),
                (b_out[NE:NE + 1, :], fc2_b.rearrange("(a n) -> a n", a=1)),
            ]
            for k in range(KT):
                loads.append((s_exp[k].rearrange("p (e o) -> p e o", o=DM), We[:, k * P:(k + 1) * P, :].rearrange("e p o -> p e o")))
            for t in range(TB):
                loads.append((b_gate[:, t, :], bg.rearrange("(a n) -> a n", a=1).to_broadcast((P, NE))))
            assert len(loads) == N_LOADS

            def load(f):
                wait(sp, moe_added, f.count(N_MOE, -2 * N_MOE + TB))
                sp.dma_start(xin[:, f.part, :, :], x_v[f.index]).then_inc(x_loaded[f.part], 16)

            load(Chunk(0, 0))
            load(Chunk(0, 1))
            for dst, src in loads:
                sp.dma_start(dst, src, allow_slow_non_contiguous=True).then_inc(w_loaded, 16)

            def store(b, t):
                wait(sp, out_ready, b.count(TB, t + 1))
                sp.dma_start(out_v[b.index][:, t, :], acc[:, t, :]).then_inc(out_stored[t], 16)

            def body(ck, has_back=True, has_front=True, has_norm=True):
                if has_back:
                    for t in range(TB):
                        store(ck.step(-1), t)
                if has_norm:
                    load(ck.step(2))

            over_chunks(sp, lambda: None, body, lambda ck: body(ck, has_norm=False))
            for t in range(TB):
                sp.wait_ge(out_stored[t], 16 * CHUNKS)

        @block.gpsimd
        def _(pool):
            pool.memset(ident[:], 0.0).then_inc(consts_set, 1)
            pool.memset(state[:], 0.0).then_inc(consts_set, 1)
            pool.memset(hist[:], 0.0).then_inc(consts_set, 1)
            pool.memset(half_neg[:], -0.5).then_inc(consts_set, 1)
            pool.memset(gates[:, :, :, NE:NE + 1], 1.0).then_inc(consts_set, 1)
            for e in range(NE):
                pool.memset(prio[:, :, e:e + 1], float(NE - e)).then_inc(consts_set, 1)
            pool.wait_ge(consts_set, 1)
            pool.affine_select(out=ident[:], in_=ident[:], compare_op=ALU.not_equal, fill=1.0, base=0,
                               pattern=[[-1, P]], channel_multiplier=1).then_inc(consts_set, 1)
            pool.wait_ge(consts_set, 6 + NE)
            pool.wait_ge(w_loaded, 16 * N_LOADS)
            pool.wait_ge(A_exp, 1)
            pool.tensor_scalar(A[:], A[:], -1.0, 1.0, ALU.mult, ALU.mult).then_inc(consts_set, 1)

            def norm(f, part):
                if part == 0:
                    pool.wait_ge(ln_chain, f.count(N_LN, N_LN))
                    wait(pool, norm_chain, f.count(N_NORM))
                    apart(pool, passed)
                    pool.tensor_scalar(rstd[:, 0, :], mv[:, :, 1], EPS, 1.0, ALU.add, ALU.mult).then_inc(norm_chain, 1)
                    pool.tensor_scalar(rstd[:, 2, :], mv[:, :, 0], -1.0, 1.0, ALU.mult, ALU.mult).then_inc(norm_chain, 1)
                elif part == 1:
                    pool.wait_ge(norm_chain, f.count(N_NORM, 2))
                    pool.tensor_tensor(rstd[:, 1, :], rstd[:, 0, :], half_neg[:], ALU.pow).then_inc(norm_chain, 1)
                elif part == 2:
                    pool.wait_ge(norm_chain, f.count(N_NORM, 3))
                    pool.tensor_tensor(rstd[:, 0, :], rstd[:, 2, :], rstd[:, 1, :], ALU.mult).then_inc(norm_chain, 1)
                else:
                    pool.wait_ge(norm_chain, f.count(N_NORM, 4))
                    t = part - 3
                    wait(pool, taps_ready, f.count(N_TAP))
                    wait(pool, conv_chain, f.count(N_CONV))
                    wait(pool, hist_saved, f.count(DT))
                    apart(pool, passed)
                    pool.tensor_scalar(xn[:, t, :], xin[:, f.part, t, :], rstd[:, 1, t:t + 1], rstd[:, 0, t:t + 1],
                                       ALU.mult, ALU.add).then_inc(norm_chain, 1)

            def clamp(f, k):
                pool.wait_ge(v_ready, f.count(DT, k + 1))
                pool.wait_ge(conv_chain, f.count(N_CONV, N_CONV))
                apart(pool, passed)
                pool.tensor_scalar(dt[:, f.part, k, :], wide[:, k, :], EXP_CAP, -BIG, ALU.min, ALU.max).then_inc(vmin_ready, 1)

            def times_u(f, k):
                pool.wait_ge(dt_ready, f.count(DT, k + 1))
                pool.tensor_tensor(wide[:, k, :], dt[:, f.part, k, :], u[:, f.part, k, :], ALU.mult).then_inc(du_ready, 1)

            def convolve(f, k, w):
                if w == 0:
                    pool.wait_ge(hist_set, f.count(DT, k + 1))
                    if k == 0:
                        wait(pool, yd_ready, f.count(TB, -TB))
                    pool.wait_ge(xc_ready, f.count(DT, k + 1))
                    apart(pool, passed)
                    pool.tensor_scalar(u[:, f.part, k, :], xc[:, k % 2, 0:CT], cw[:, k, 0:1], cb[:, k:k + 1],
                                       ALU.mult, ALU.add).then_inc(conv_chain, 1)
                else:
                    i = k * (TAPS - 1) + w - 1
                    pool.wait_ge(taps_ready, f.count(N_TAP, i + 1))
                    pool.wait_ge(conv_chain, f.count(N_CONV, k * TAPS + w))
                    pool.tensor_tensor(u[:, f.part, k, :], u[:, f.part, k, :], dt[:, f.part, i % DT, :], ALU.add).then_inc(conv_chain, 1)

            def gate_y(b, t):
                pool.wait_ge(yd_ready, b.count(TB, t + 1))
                pool.wait_ge(sz_ready, b.count(1, 1))
                cols = slice(t * P, (t + 1) * P)
                pool.tensor_tensor(wide[:, :, cols], wide[:, :, cols], sz[:, :, cols], ALU.mult).then_inc(yg_ready, 1)

            def scale_b(ck, n, t):
                if n == 0:
                    pool.wait_ge(duT_ready, ck.count(TB, t + 1))
                    pool.wait_ge(bc_ready, ck.count(1, 1))
                    apart(pool, passed)
                if t == 0:
                    wait(pool, x_filled, ck.count(STEPS, DT * (n - 1)))
                    apart(pool, passed)
                pool.tensor_scalar(xb[:, n % 2, t, :], duT[:, ck.part, t, :], bc[:, ck.part, t, R + n:R + n + 1],
                                   1.0, ALU.mult, ALU.mult).then_inc(xb_ready, 1)

            def save_state(ck, n):
                wait(pool, scan_done, ck.count(STEPS, DT * (n + 1)))
                apart(pool, passed)
                pool.tensor_copy(state[:, slot_after(ck), n, :], h[:, n % 2, :, CT - 1]).then_inc(state_saved, 1)

            def steps(ck, has_back=True, has_front=True, has_norm=True, has_steps=True):
                f, b, g = ck.step(1), ck.step(-1), ck.step(2)
                for q in range(STEPS):
                    n = q // DT
                    if has_steps:
                        if n + 1 < NSTATE:
                            scale_b(ck, n + 1, q % DT)
                        if q % DT == 1:
                            if n > 0:
                                save_state(ck, n - 1)
                            elif not (ck.is_int() and ck.index == 0):
                                save_state(b, NSTATE - 1)
                    if has_back:
                        for t in range(TB):
                            if q == Q_YG[t][0] + 3:
                                gate_y(b, t)
                    if has_norm and 0 <= q - Q_NORM < 3 + TB:
                        norm(g, q - Q_NORM)
                    if has_front:
                        for k in range(DT):
                            if 0 <= q - Q_CONV[k] < TAPS:
                                convolve(f, k, q - Q_CONV[k])
                            if q == Q_MIN[k]:
                                clamp(f, k)
                            if q == Q_DTU[k]:
                                times_u(f, k)
                        if 0 <= q - Q_XB0 < TB:
                            scale_b(f, 0, q - Q_XB0)

            before_first, behind_last = around(steps)
            over_chunks(pool, before_first, steps, behind_last)

        @block.scalar
        def _(act):
            act.wait_ge(w_loaded, 16 * N_LOADS)
            act.activation(A[:], A[:], ACT.Exp).then_inc(A_exp, 1)
            for i, (_, dst, src) in enumerate(prep_jobs):
                act.wait_ge(prep_filled, i + 1)
                act.copy(dst, src(ps_x[i % 2])).then_inc(prep_copied, 1)
            act.copy(w_gate[:, 0, :, :], s_gate).then_inc(split_done, 1)
            for k in range(KT):
                act.copy(w_exp[:, 0, k, :], s_exp[k]).then_inc(split_done, 1)
            act.wait_ge(split_done, N_SPLIT)

            def load_exp_and_ln():
                act.add_instruction(mybir.InstLoadActFuncSet(name=nc.get_next_instruction_name(), engine=act.engine,
                                                             act_func_set_id=EXP_AND_LN))

            def take(f, job):
                act.wait_ge(front_filled, f.count(NF, FRONT_AT[job] + 1))
                return ps_f[front_bank(f, job)]

            def front(f, q):
                for k in range(KT):
                    if q == Q_XNT[k][-1] + 1:
                        if k == 0:
                            wait(act, side_filled, f.step(-2).count(NS, NS - NB))
                        bank = take(f, (XNT, k))
                        act.copy(xnT[:, f.part, 0, k, :], bank[:]).then_inc(xnT_ready, 1)
                for k in range(DT):
                    if q == Q_XC[k][-1] + 1:
                        bank = take(f, (XC, k))
                        if k >= 2:
                            act.wait_ge(conv_chain, f.count(N_CONV, TAPS * (k - 2) + 1))
                            act.wait_ge(hist_saved, f.count(DT, k - 1))
                            act.wait_ge(taps_ready, f.count(N_TAP, (TAPS - 1) * (k - 1)))
                        act.activation(xc[:, k % 2, HIST:], bank[:], ACT.Identity, bias=b_xz[:, k:k + 1]).then_inc(xc_ready, 1)
                    if q == Q_CONV[k] - 1:
                        act.wait_ge(xc_ready, f.count(DT, k + 1))
                        act.wait_ge(hist_set, f.count(DT, k + 1))
                        if k == 0:
                            wait(act, dA_ready, f.count(STEPS, -STEPS))
                    if 0 < q - Q_CONV[k] + 2 < TAPS:
                        w = q - Q_CONV[k] + 2
                        i = k * (TAPS - 1) + w - 1
                        if i >= DT:
                            before = i - DT
                            act.wait_ge(conv_chain, f.count(N_CONV, before // (TAPS - 1) * TAPS + before % (TAPS - 1) + 2))
                        act.activation(dt[:, f.part, i % DT, :], xc[:, k % 2, w:w + CT], ACT.Identity,
                                       scale=cw[:, k, w:w + 1]).then_inc(taps_ready, 1)
                if q == Q_SILU:
                    act.wait_ge(conv_chain, f.count(N_CONV, N_CONV))
                    act.activation(u[:, f.part, :, :], u[:, f.part, :, :], ACT.Silu).then_inc(u_ready, 1)
                if q == Q_E2:
                    act.wait_ge(gate_chain, f.count(N_GATE, len(Q_TOP2)))
                    act.activation(gs[:, 4, :], gs[:, 3, :], ACT.Exp).then_inc(e2_ready, 1)
                if q == Q_XD[-1] + 1:
                    bank = take(f, (XDBL, 0))
                    act.copy(xdT[:], bank[0:XD, :]).then_inc(xd_ready, 1)
                if q == Q_BC[0] + 1:
                    bank = take(f, (BC, 0))
                    wait(act, y_added, f.count(STEPS, -STEPS))
                    act.copy(bc[:, f.part, :, :], bank[:, 0:TB * XD].rearrange("p (t x) -> p t x", t=TB)).then_inc(bc_ready, 1)
                for k in range(DT):
                    if q == Q_DT[k][-1] + 1:
                        bank = take(f, (DELTA, k))
                        if k == 0:
                            wait(act, out_ready, f.count(TB, -TB))
                        act.activation(wide[:, k, :], bank[:], ACT.Identity, bias=b_dt[:, k:k + 1]).then_inc(v_ready, 1)
                for k in range(DT):
                    if q == Q_SP[k]:
                        act.wait_ge(vmin_ready, f.count(DT, k + 1))
                        act.activation(dt[:, f.part, k, :], dt[:, f.part, k, :], ACT.Exp).then_inc(e_ready, 1)
                    if q == Q_SP[k] + 1:
                        act.wait_ge(e_ready, f.count(DT, k + 1))
                        act.activation(dt[:, f.part, k, :], dt[:, f.part, k, :], ACT.Ln, bias=1.0).then_inc(ln_ready, 1)
                for k in range(TB):
                    if q == Q_DUT[k][-1] + 1:
                        bank = take(f, (DUT, k))
                        if k == 0:
                            wait(act, xb_ready, f.count(NSTATE * TB, -NSTATE * TB))
                        act.copy(duT[:, f.part, k, :], bank[:]).then_inc(duT_ready, 1)

            def decay(ck, q):
                n, k = q // DT, q % DT
                if q == 0:
                    act.wait_ge(dt_ready, ck.count(DT, DT))
                wait(act, scan_done, ck.count(STEPS, q - DT + 1))
                act.activation(dA[:, k, :], dt[:, ck.part, k, :], ACT.Exp, scale=A[:, k, n:n + 1]).then_inc(dA_ready, 1)

            def gate_z(ck, q):
                for k in range(DT):
                    if q == Q_Z[k][-1] + 1:
                        job = (Z, k)
                        bank = side_bank(ck, job)
                        act.wait_ge(side_filled, side_count(ck, job))
                        if k == 0:
                            wait(act, yg_ready, ck.count(TB))
                        act.activation(sz[:, k, :], ps_s[bank][:], ACT.Identity,
                                       bias=b_xz[:, DT + k:DT + k + 1]).then_inc(z_ready, 1)
                if q == Q_SILU:
                    act.wait_ge(z_ready, ck.count(DT, DT))
                    act.activation(sz[:], sz[:], ACT.Silu).then_inc(sz_ready, 1)

            def steps(ck, has_back=True, has_front=True, has_norm=True, has_steps=True):
                f, b, g = ck.step(1), ck.step(-1), ck.step(2)
                for q in range(STEPS):
                    if has_steps:
                        decay(ck, q)
                    if has_front:
                        front(f, q)
                    if has_steps:
                        gate_z(ck, q)
                        for k in range(DT):
                            if q == Q_UD[k]:
                                act.wait_ge(du_ready, ck.count(DT, DT))
                                act.activation(u[:, ck.part, k, :], u[:, ck.part, k, :], ACT.Identity,
                                               scale=d_col[:, k:k + 1]).then_inc(ud_ready, 1)
                    if q == Q_SILU and (has_front or has_steps):
                        load_exp_and_ln()
                    if has_back and q == Q_GT[0] + 1:
                        act.wait_ge(side_filled, side_count(ck, (GT, 0)))
                        act.copy(gT[:], ps_s[side_bank(ck, (GT, 0))][0:NE + 1, :]).then_inc(gT_ready, 1)

            act.wait_ge(consts_set, N_CONSTS)
            before_first, behind_last = around(steps)
            over_chunks(act, before_first, steps, behind_last)

        @block.vector
        def _(dve):
            def stats(f, q):
                for t in range(TB):
                    if q == Q_STATS[t]:
                        if t == 0:
                            dve.wait_ge(x_loaded[f.part], f.turn * 16 + 16)
                        dve.bn_stats(stat[:, t, :], xin[:, f.part, t, :]).then_inc(ln_chain, 1)
                if q == Q_AGGR:
                    dve.wait_ge(ln_chain, f.count(N_LN, TB))
                    wait(dve, norm_chain, f.count(N_NORM))
                    apart(dve, passed)
                    for t in range(TB):
                        dve.bn_aggr(mv[:, t, :], stat[:, t, :]).then_inc(ln_chain, 1)

            def top2(f, q):
                if q not in Q_TOP2 + Q_SHARE:
                    return
                n = (Q_TOP2 + Q_SHARE).index(q)

                def wide_of(col):
                    return gs[:, col, :].unsqueeze(2).to_broadcast([P, TB, NE])

                lg, eq, r, k1, l2, k2 = (gw[:, i, :, :] for i in range(6))
                if n == 0:
                    dve.wait_ge(front_filled, f.count(NF, FRONT_AT[(LOGIT, 0)] + 1))
                    wait(dve, e2_ready, f.count(1))
                wait(dve, gate_chain, f.count(N_GATE, n))
                if n == len(Q_TOP2):
                    dve.wait_ge(e2_ready, f.count(1, 1))
                if n == N_GATE - 1:
                    wait(dve, gT_ready, f.count(1, -1))
                logits = ps_f[front_bank(f, (LOGIT, 0))][:, 0:TB * NE].rearrange("p (t e) -> p t e", t=TB)
                links = (
                    lambda: dve.tensor_tensor(lg, logits, b_gate[:], ALU.add),
                    lambda: dve.tensor_reduce(gs[:, 0, :], lg, AX_X, ALU.max),
                    lambda: dve.tensor_tensor(eq, lg, wide_of(0), ALU.is_equal),
                    lambda: dve.tensor_tensor(r, eq, prio[:], ALU.mult),
                    lambda: dve.tensor_reduce(gs[:, 1, :], r, AX_X, ALU.max),
                    lambda: dve.tensor_tensor(k1, r, wide_of(1), ALU.is_equal),
                    lambda: dve.scalar_tensor_tensor(l2, k1, -BIG, lg, ALU.mult, ALU.add),
                    lambda: dve.tensor_reduce(gs[:, 2, :], l2, AX_X, ALU.max),
                    lambda: dve.tensor_tensor(eq, l2, wide_of(2), ALU.is_equal),
                    lambda: dve.tensor_tensor(r, eq, prio[:], ALU.mult),
                    lambda: dve.tensor_reduce(gs[:, 1, :], r, AX_X, ALU.max),
                    lambda: dve.tensor_tensor(k2, r, wide_of(1), ALU.is_equal),
                    lambda: dve.tensor_tensor(gs[:, 3, :], gs[:, 2, :], gs[:, 0, :], ALU.subtract),
                    lambda: dve.tensor_scalar(gs[:, 5, :], gs[:, 4, :], 1.0, None, ALU.add),
                    lambda: dve.reciprocal(gs[:, 6, :], gs[:, 5, :]),
                    lambda: dve.tensor_tensor(gs[:, 7, :], gs[:, 4, :], gs[:, 6, :], ALU.mult),
                    lambda: dve.tensor_tensor(eq, k1, wide_of(6), ALU.mult),
                    lambda: dve.tensor_tensor(r, k2, wide_of(7), ALU.mult),
                    lambda: dve.tensor_tensor(gates[:, f.part, :, 0:NE], eq, r, ALU.add),
                )
                assert len(links) == N_GATE
                links[n]().then_inc(gate_chain, 1)

            def front(f, q):
                top2(f, q)
                for k in range(KT):
                    if q == Q_XNT[k][-1] + 2:
                        bank = front_bank(f, (XNT, k))
                        dve.wait_ge(front_filled, f.count(NF, FRONT_AT[(XNT, k)] + 1))
                        dve.wait_ge(xnT_ready, f.count(KT, k + 1))
                        dve.tensor_tensor(xnT[:, f.part, 1, k, :], ps_f[bank][:], xnT[:, f.part, 0, k, :].bitcast(F32),
                                          ALU.subtract).then_inc(xnL_ready, 1)
                for k in range(DT):
                    if q == Q_XC[k][0]:
                        if k < 2:
                            dve.wait_ge(front_filled, f.count(NF, FRONT_AT[(XNT, KT - 1)] + 1))
                        else:
                            dve.wait_ge(conv_chain, f.count(N_CONV, TAPS * (k - 2) + 1))
                            dve.wait_ge(taps_ready, f.count(N_TAP, (TAPS - 1) * (k - 1)))
                        wait(dve, hist_saved, f.count(DT, max(k - 1, 0)))
                        dve.tensor_copy(xc[:, k % 2, 0:HIST], hist[:, slot_before(f), k, :]).then_inc(hist_set, 1)
                    if q == Q_XC[k][-1] + 2:
                        dve.wait_ge(xc_ready, f.count(DT, k + 1))
                        dve.tensor_copy(hist[:, slot_after(f), k, :], xc[:, k % 2, CT:CT + HIST]).then_inc(hist_saved, 1)
                for k in range(DT):
                    if q == Q_MAX[k]:
                        dve.wait_ge(ln_ready, f.count(DT, k + 1))
                        dve.tensor_tensor(dt[:, f.part, k, :], dt[:, f.part, k, :], wide[:, k, :], ALU.max).then_inc(dt_ready, 1)

            def back(ck, q):
                b = ck.step(-1)
                for t in range(TB):
                    if q == Q_YG[t][-1] + 1:
                        job = (YG, t)
                        bank = side_bank(ck, job)
                        dve.wait_ge(side_filled, side_count(ck, job))
                        dve.wait_ge(ud_ready, b.count(DT, DT))
                        cols = slice(t * P, (t + 1) * P)
                        dve.tensor_tensor(wide[:, :, cols], ps_s[bank][:].rearrange("p (k t) -> p k t", k=DT),
                                          u[:, b.part, :, cols], ALU.add).then_inc(yd_ready, 1)
                for t in range(TB):
                    if q == Q_OUT[t][-1] + 1:
                        job = (OUT, t)
                        dve.wait_ge(side_filled, side_count(ck, job))
                        dve.wait_ge(moe_added, b.count(N_MOE, N_MOE))
                        dve.tensor_tensor(acc[:, t, :], ps_s[side_bank(ck, job)][:, 0:DM], acc[:, t, :], ALU.add).then_inc(out_ready, 1)

            def experts(ck, q):
                for i in range(N_MOE):
                    if q == min(Q_MOE[i][0] + 1, STEPS - 1):
                        e, t = i // TB, i % TB
                        if e == 0:
                            wait(dve, out_stored[t], ck.count(16))
                            if t == 0:
                                dve.wait_ge(gate_chain, ck.count(N_GATE, N_GATE))
                        else:
                            dve.wait_ge(moe_added, ck.count(N_MOE, i - TB + 1))
                        dve.wait_ge(side_filled, side_count(ck, (MOE, i)))
                        dve.scalar_tensor_tensor(acc[:, t, :], ps_s[side_bank(ck, (MOE, i))][:, 0:DM],
                                                 gates[:, ck.part, t, e:e + 1],
                                                 xin[:, ck.part, t, :] if e == 0 else acc[:, t, :],
                                                 ALU.mult, ALU.add).then_inc(moe_added, 1)

            def scan(ck, q):
                n, k = q // DT, q % DT
                if k == 0:
                    wait(dve, h_filled, ck.count(STEPS, DT * (n - 1)))
                    wait(dve, state_saved, ck.count(NSTATE, n - 1))
                dve.wait_ge(dA_ready, ck.count(STEPS, q + 1))
                dve.wait_ge(x_filled, ck.count(STEPS, q + 1))
                dve.tensor_tensor_scan(h[:, n % 2, k, :], dA[:, k, :], ps_x[q % 2][:],
                                       state[:, slot_before(ck), n, k:k + 1], ALU.mult, ALU.add).then_inc(scan_done, 1)

            def add_y(ck, n, t):
                i = DT * n + t
                dve.wait_ge(h_filled, ck.count(STEPS, i + 1))
                if n == 0:
                    if t == 0:
                        dve.wait_ge(bc_ready, ck.count(1, 1))
                    wait(dve, side_filled, side_count(ck, (YG, t)))
                    dve.tensor_scalar(yT[:, t, :], ps_h[t % 2][:], bc[:, ck.part, t, R + NSTATE:R + NSTATE + 1],
                                      None, ALU.mult).then_inc(y_added, 1)
                else:
                    dve.wait_ge(y_added, ck.count(STEPS, i - TB + 1))
                    dve.scalar_tensor_tensor(yT[:, t, :], ps_h[t % 2][:],
                                             bc[:, ck.part, t, R + NSTATE + n:R + NSTATE + n + 1],
                                             yT[:, t, :], ALU.mult, ALU.add).then_inc(y_added, 1)

            def steps(ck, has_back=True, has_front=True, has_norm=True, has_steps=True):
                f, b, g = ck.step(1), ck.step(-1), ck.step(2)
                for q in range(STEPS):
                    if has_steps:
                        scan(ck, q)
                    if q >= DT:
                        if has_steps:
                            add_y(ck, q // DT - 1, q % DT)
                    elif has_back or (has_steps and not (ck.is_int() and ck.index == 0)):
                        add_y(b, NSTATE - 1, q)
                    if has_norm:
                        stats(g, q)
                    if has_front:
                        front(f, q)
                    if has_back:
                        back(ck, q)
                    if has_steps:
                        experts(ck, q)

            dve.wait_ge(w_loaded, 16 * N_LOADS)
            for i, half in ((i, half) for i in range(KT) for half in range(2)):
                job = JOIN_AT + 2 * i + half
                dve.wait_ge(prep_copied, job + 1)
                cols = slice(half * 512, (half + 1) * 512)
                dve.tensor_tensor(w_xz[:, 1, i, cols], ps_x[job % 2][:], w_xz[:, 0, i, cols].bitcast(F32),
                                  ALU.subtract).then_inc(prep_split, 1)
            dve.wait_ge(split_done, 1 + KT)
            dve.tensor_tensor(w_gate[:, 1, :, :], s_gate, w_gate[:, 0, :, :].bitcast(F32), ALU.subtract).then_inc(split_done, 1)
            for k in range(KT):
                dve.tensor_tensor(w_exp[:, 1, k, :], s_exp[k], w_exp[:, 0, k, :].bitcast(F32),
                                  ALU.subtract).then_inc(split_done, 1)
            dve.wait_ge(split_done, N_SPLIT)
            dve.wait_ge(consts_set, N_CONSTS)
            before_first, behind_last = around(steps)
            over_chunks(dve, before_first, steps, behind_last)

        @block.tensor
        def _(pe):
            pe.wait_ge(w_loaded, 16 * N_LOADS)
            pe.wait_ge(consts_set, N_CONSTS)
            for i, (fill, _, _) in enumerate(prep_jobs):
                wait(pe, prep_copied, i - 1)
                wait(pe, prep_split, min(max(i - 1 - JOIN_AT, 0), 2 * KT))
                last = fill(pe, ps_x[i % 2])
                last.then_inc(prep_filled, 1)
            pe.wait_ge(prep_copied, len(prep_jobs))
            pe.wait_ge(split_done, N_SPLIT)

            def mm(out, lhsT, rhs, k, n):
                return pe.matmul(out, lhsT, rhs, start=k == 0, stop=k == n - 1)

            def mm_halves(out, lhsT, rhs, part=0, parts=1):
                passes = [(a, b, i) for i in range(KT) for a, b in ((0, 0), (0, 1), (1, 0))]
                size = len(passes) // parts
                for n in range(part * size, (part + 1) * size):
                    a, b, i = passes[n]
                    last = mm(out, lhsT(a, i), rhs(b, i), n, len(passes))
                return last

            def xn_rows(part, t):
                return lambda half, i: xnT[:, part, half, i, t * P:(t + 1) * P]

            def inner(of, bank, e, part):
                return mm_halves(bank[:], lambda half, i: w_xz[:, half, i, e * P:(e + 1) * P],
                                 lambda half, i: xnT[:, of.part, half, i, :], part, 2)

            def fill_front(f, job, part):
                kind, k = job
                bank = ps_f[front_bank(f, job)]
                if part == 0:
                    before = two_before(f, job, FRONT, FRONT_AT, front_ran)
                    if before:
                        wait(pe, *front_taken(*before))
                if kind == XNT:
                    pe.wait_ge(norm_chain, f.count(N_NORM, N_NORM))
                    for t in range(TB):
                        last = pe.transpose(bank[:, t * P:(t + 1) * P], xn[:, t, k * P:(k + 1) * P], ident[:])
                elif kind == LOGIT:
                    for t in range(TB):
                        last = mm_halves(bank[:, t * NE:(t + 1) * NE], xn_rows(f.part, t), lambda half, i: w_gate[:, half, i, :])
                elif kind == XC:
                    if k == 0 and part == 0:
                        pe.wait_ge(xnT_ready, f.count(KT, KT))
                        pe.wait_ge(xnL_ready, f.count(KT, KT))
                    last = inner(f, bank, k, part)
                elif kind == XDBL:
                    if part == 0:
                        pe.wait_ge(u_ready, f.count(1, 1))
                    last = mm(bank[0:XD, :], w_xd[:, part, :], u[:, f.part, part, :], part, DT)
                elif kind == BC:
                    pe.wait_ge(xd_ready, f.count(1, 1))
                    apart(pe, passed)
                    for t in range(TB):
                        last = pe.transpose(bank[:, t * XD:(t + 1) * XD], xdT[:, t * P:(t + 1) * P], ident[0:XD, 0:XD])
                elif kind == DELTA:
                    last = mm(bank[:], w_dt[:, k * P:(k + 1) * P], xdT[0:R, :], 0, 1)
                else:
                    pe.wait_ge(du_ready, f.count(DT, DT))
                    for i in range(DT):
                        last = pe.transpose(bank[:, i * P:(i + 1) * P], wide[:, i, k * P:(k + 1) * P], ident[:])
                if part == len(FRONT_PLACES[job]) - 1:
                    last.then_inc(front_filled, 1)

            def fill_side(ck, job, part):
                kind, k = job
                b = ck.step(-1)
                bank = ps_s[side_bank(ck, job)]
                if part == 0:
                    before = two_before(ck, job, SIDE, SIDE_AT, side_ran)
                    if before:
                        wait(pe, *side_taken(*before))
                if kind == GT:
                    pe.wait_ge(gate_chain, b.count(N_GATE, N_GATE))
                    for t in range(TB):
                        last = pe.transpose(bank[0:NE + 1, t * P:(t + 1) * P], gates[:, b.part, t, :], ident[:])
                elif kind == YG:
                    pe.wait_ge(y_added, b.count(STEPS, STEPS - TB + k + 1))
                    for i in range(DT):
                        last = pe.transpose(bank[:, i * P:(i + 1) * P], yT[:, k, i * P:(i + 1) * P], ident[:])
                elif kind == OUT:
                    if part == 0:
                        pe.wait_ge(yg_ready, b.count(TB, k + 1))
                        pe.wait_ge(gT_ready, b.count(1, 1))
                    for i in ((0, 1), (2, 3), ())[part]:
                        mm(bank[:, 0:DM], wide[:, i, k * P:(k + 1) * P], w_out[:, i, :], i, DT + 1)
                    if part < 2:
                        return
                    last = mm(bank[:, 0:DM], gT[:, k * P:(k + 1) * P], b_out[:], DT, DT + 1)
                elif kind == Z:
                    last = inner(ck, bank, DT + k, part)
                else:
                    e, t = k // TB, k % TB
                    last = mm_halves(bank[:, 0:DM], xn_rows(ck.part, t),
                                     lambda half, i: w_exp[:, half, i, e * DM:(e + 1) * DM])
                if part == len(SIDE_PLACES[job]) - 1:
                    last.then_inc(side_filled, 1)

            def turn_x(ck, q):
                n, k = q // DT, q % DT
                if k == 0:
                    pe.wait_ge(xb_ready, ck.count(NSTATE * TB, TB * (n + 1)))
                wait(pe, scan_done, ck.count(STEPS, q - 1))
                for t in range(TB):
                    last = pe.transpose(ps_x[q % 2][:, t * P:(t + 1) * P], xb[:, n % 2, t, k * P:(k + 1) * P], ident[:])
                last.then_inc(x_filled, 1)

            def turn_h(ck, n, t):
                i = DT * n + t
                if t == 0:
                    pe.wait_ge(scan_done, ck.count(STEPS, DT * (n + 1)))
                wait(pe, y_added, ck.count(STEPS, i - 1))
                for k in range(DT):
                    last = pe.transpose(ps_h[t % 2][:, k * P:(k + 1) * P], h[:, n % 2, k, t * P:(t + 1) * P], ident[:])
                last.then_inc(h_filled, 1)

            def steps(ck, has_back=True, has_front=True, has_norm=True, has_steps=True):
                f, b, g = ck.step(1), ck.step(-1), ck.step(2)
                for q in range(STEPS):
                    if has_steps:
                        turn_x(ck, q)
                    if q >= DT:
                        if has_steps:
                            turn_h(ck, q // DT - 1, q % DT)
                    elif has_back or (has_steps and not (ck.is_int() and ck.index == 0)):
                        turn_h(b, NSTATE - 1, q)
                    for job in FRONT if has_front else ():
                        for part, at in enumerate(FRONT_PLACES[job]):
                            if at == q:
                                fill_front(f, job, part)
                    for job in SIDE if has_back or has_steps else ():
                        for part, at in enumerate(SIDE_PLACES[job]):
                            if at == q:
                                if side_ran(ck, job):
                                    fill_side(ck, job, part)

            before_first, behind_last = around(steps)
            over_chunks(pe, before_first, steps, behind_last)


_INS = ['x', 'fc1_w', 'fc1_b', 'in_proj_w', 'conv_w', 'conv_b', 'x_proj_w', 'dt_proj_w', 'dt_proj_b',
        'A_log', 'D', 'out_proj_w', 'fc2_w', 'fc2_b']
_INS = ['L0_attn_' + n for n in _INS] + ['L0_ffn_We', 'L0_ffn_be', 'L0_ffn_Wg', 'L0_ffn_bg']


def kernel(**inputs):
    import numpy as _np
    import concourse.bacc as _bacc
    from concourse import mybir as _mybir
    from concourse.bass_utils import run_bass_kernel_spmd as _run

    nc = _bacc.Bacc("TRN2", target_bir_lowering=False, num_devices=1)
    arrays, args = {}, []
    for name in _INS:
        a = _np.ascontiguousarray(inputs[name])
        arrays[f"in_{name}_dram"] = a
        args.append(nc.dram_tensor(f"in_{name}_dram", a.shape, _mybir.dt.from_np(a.dtype), kind="ExternalInput").ap())
    shape = inputs['L0_attn_x'].shape
    args.append(nc.dram_tensor("out_0_dram", shape, _mybir.dt.float32, kind="ExternalOutput").ap())
    mamba_moe_kernel(nc, *args)
    r = _run(nc, [arrays], core_ids=[0])
    return r.results[0]["out_0_dram"]
```
